# Optimizing a Trainium2 kernel written in Bass

```python
import numpy as np
import jax
import jax.numpy as jnp

def _softmax(x, axis=-1):
    return jax.nn.softmax(x, axis=axis)

def _gelu(x):
    return jax.nn.gelu(x, approximate=True)

def _silu(x):
    return jax.nn.silu(x)

def _sigmoid(x):
    return jax.nn.sigmoid(x)

def _layernorm(x, axis=-1, eps=1e-05):
    m = jnp.mean(x, axis=axis, keepdims=True)
    v = jnp.var(x, axis=axis, keepdims=True)
    return (x - m) / jnp.sqrt(v + eps)

def _scatter_add(tgt, idx, src, axis=0):
    return tgt.at[idx].add(src)

def _segment_sum(src, seg, n):
    return jax.ops.segment_sum(src, seg, n)
kernel_name = 'mk_sandwich_d2_jaxref_r8_217b43'

def setup_inputs(seed: int=0):
    np.random.seed(seed)
    _w = jnp.asarray

    def _L0_attn_setup():
        import jax, jax.numpy as jnp
        import numpy as np
        HIDDEN = 256
        NUM_HEADS = 16
        HEAD_DIM = 128
        INNER = NUM_HEADS * HEAD_DIM
        ROPE_BASE = 10000.0

        def apply_rope(x):
            B, H, S, D = x.shape
            inv_freq = 1.0 / ROPE_BASE ** (jnp.arange(0, D, 2, dtype=jnp.float32) / D)
            t = jnp.arange(S, dtype=jnp.float32)
            freqs = t[:, None] * inv_freq[None, :]
            cos = jnp.concatenate([jnp.cos(freqs)] * 2, -1)
            sin = jnp.concatenate([jnp.sin(freqs)] * 2, -1)
            x1, x2 = (x[..., :D // 2], x[..., D // 2:])
            rotated = jnp.concatenate([-x2, x1], axis=-1)
            return x * cos[None, None] + rotated * sin[None, None]
        key = jax.random.key(seed)
        ks = jax.random.split(key, 9)
        s = 1.0 / np.sqrt(HIDDEN)
        return {'hidden_states': jax.random.normal(ks[0], (2, 256, HIDDEN), jnp.float32), 'Wq': jax.random.uniform(ks[1], (INNER, HIDDEN), jnp.float32, -s, s), 'bq': jax.random.uniform(ks[2], (INNER,), jnp.float32, -s, s), 'Wk': jax.random.uniform(ks[3], (INNER, HIDDEN), jnp.float32, -s, s), 'bk': jax.random.uniform(ks[4], (INNER,), jnp.float32, -s, s), 'Wv': jax.random.uniform(ks[5], (INNER, HIDDEN), jnp.float32, -s, s), 'bv': jax.random.uniform(ks[6], (INNER,), jnp.float32, -s, s), 'Wo': jax.random.uniform(ks[7], (HIDDEN, INNER), jnp.float32, -s, s), 'bo': jax.random.uniform(ks[8], (HIDDEN,), jnp.float32, -s, s)}
    _L0_attn_in = _L0_attn_setup()

    def _L0_ffn_setup():
        import jax, jax.numpy as jnp
        import numpy as np
        EPS = 1e-08

        def _quantize(w):
            gamma = jnp.mean(jnp.abs(w))
            return jnp.clip(jnp.round(w / (gamma + EPS)), -1.0, 1.0)

        def _bitlinear(x, w):
            return jnp.matmul(x, _quantize(w).T)
        key = jax.random.key(seed)
        k1, k2, k3, k4 = jax.random.split(key, 4)
        d, h = (256, 704)
        x = jax.random.normal(k1, (4, 256, d), dtype=jnp.float32)
        w1 = jax.random.normal(k2, (h, d), dtype=jnp.float32)
        w2 = jax.random.normal(k3, (h, d), dtype=jnp.float32)
        w3 = jax.random.normal(k4, (d, h), dtype=jnp.float32)
        return {'x': x, 'w1': w1, 'w2': w2, 'w3': w3}
    _L0_ffn_in = _L0_ffn_setup()

    def _L1_attn_setup():
        import jax, jax.numpy as jnp
        import numpy as np
        DIM = 256
        N_HEADS = 32
        N_KV_HEADS = 8
        HEAD_DIM = DIM // N_HEADS
        ROPE_BASE = 10000.0
        BATCH = 2
        SEQ = 256

        def _rope_cos_sin(seq_len, dtype=jnp.float32):
            inv_freq = 1.0 / ROPE_BASE ** (jnp.arange(0, HEAD_DIM, 2, dtype=jnp.float32) / HEAD_DIM)
            pos = jnp.arange(seq_len, dtype=jnp.float32)
            freqs = pos[:, None] * inv_freq[None, :]
            return (jnp.cos(freqs).astype(dtype), jnp.sin(freqs).astype(dtype))

        def _apply_rope(x, cos, sin):
            cos = cos[None, None, :, :]
            sin = sin[None, None, :, :]
            x_even = x[..., ::2]
            x_odd = x[..., 1::2]
            rot_even = x_even * cos - x_odd * sin
            rot_odd = x_even * sin + x_odd * cos
            out = jnp.stack((rot_even, rot_odd), axis=-1)
            return out.reshape(x.shape)
        key = jax.random.key(seed)
        ks = jax.random.split(key, 5)
        s = 0.02
        return {'x': jax.random.normal(ks[0], (BATCH, SEQ, DIM), dtype=jnp.float32), 'wq': jax.random.normal(ks[1], (DIM, N_HEADS * HEAD_DIM), dtype=jnp.float32) * s, 'wk': jax.random.normal(ks[2], (DIM, N_KV_HEADS * HEAD_DIM), dtype=jnp.float32) * s, 'wv': jax.random.normal(ks[3], (DIM, N_KV_HEADS * HEAD_DIM), dtype=jnp.float32) * s, 'wo': jax.random.normal(ks[4], (DIM, DIM), dtype=jnp.float32) * s}
    _L1_attn_in = _L1_attn_setup()

    def _L1_ffn_setup():
        import jax, jax.numpy as jnp
        import numpy as np
        DIM_IN = 256
        DIM_HIDDEN = 1024
        key = jax.random.key(seed)
        k_x, k_g, k_u, k_d = jax.random.split(key, 4)
        s_in = 1.0 / np.sqrt(DIM_IN)
        s_hid = 1.0 / np.sqrt(DIM_HIDDEN)
        x = jax.random.normal(k_x, (4, 256, DIM_IN), dtype=jnp.float32)
        w_gate = jax.random.uniform(k_g, (DIM_HIDDEN, DIM_IN), jnp.float32, -s_in, s_in)
        w_up = jax.random.uniform(k_u, (DIM_HIDDEN, DIM_IN), jnp.float32, -s_in, s_in)
        w_down = jax.random.uniform(k_d, (DIM_IN, DIM_HIDDEN), jnp.float32, -s_hid, s_hid)
        return {'x': x, 'w_gate': w_gate, 'w_up': w_up, 'w_down': w_down}
    _L1_ffn_in = _L1_ffn_setup()
    _d = {'L0_attn_hidden_states': _L0_attn_in['hidden_states'], 'L0_attn_Wq': _L0_attn_in['Wq'], 'L0_attn_bq': _L0_attn_in['bq'], 'L0_attn_Wk': _L0_attn_in['Wk'], 'L0_attn_bk': _L0_attn_in['bk'], 'L0_attn_Wv': _L0_attn_in['Wv'], 'L0_attn_bv': _L0_attn_in['bv'], 'L0_attn_Wo': _L0_attn_in['Wo'], 'L0_attn_bo': _L0_attn_in['bo'], 'L0_ffn_w1': _L0_ffn_in['w1'], 'L0_ffn_w2': _L0_ffn_in['w2'], 'L0_ffn_w3': _L0_ffn_in['w3'], 'L1_attn_wq': _L1_attn_in['wq'], 'L1_attn_wk': _L1_attn_in['wk'], 'L1_attn_wv': _L1_attn_in['wv'], 'L1_attn_wo': _L1_attn_in['wo'], 'L1_ffn_w_gate': _L1_ffn_in['w_gate'], 'L1_ffn_w_up': _L1_ffn_in['w_up'], 'L1_ffn_w_down': _L1_ffn_in['w_down']}
    _x0 = _d['L0_attn_hidden_states']
    _d['L0_attn_hidden_states'] = jax.random.normal(jax.random.fold_in(jax.random.key(seed), 1), (2, 1024, 256), dtype=_x0.dtype)
    del _x0
    return _d

def reference(L0_attn_hidden_states, L0_attn_Wq, L0_attn_bq, L0_attn_Wk, L0_attn_bk, L0_attn_Wv, L0_attn_bv, L0_attn_Wo, L0_attn_bo, L0_ffn_w1, L0_ffn_w2, L0_ffn_w3, L1_attn_wq, L1_attn_wk, L1_attn_wv, L1_attn_wo, L1_ffn_w_gate, L1_ffn_w_up, L1_ffn_w_down):

    def _L0_attn_ref(hidden_states, Wq, bq, Wk, bk, Wv, bv, Wo, bo):
        import jax, jax.numpy as jnp
        import numpy as np
        HIDDEN = 256
        NUM_HEADS = 16
        HEAD_DIM = 128
        INNER = NUM_HEADS * HEAD_DIM
        ROPE_BASE = 10000.0

        def apply_rope(x):
            B, H, S, D = x.shape
            inv_freq = 1.0 / ROPE_BASE ** (jnp.arange(0, D, 2, dtype=jnp.float32) / D)
            t = jnp.arange(S, dtype=jnp.float32)
            freqs = t[:, None] * inv_freq[None, :]
            cos = jnp.concatenate([jnp.cos(freqs)] * 2, -1)
            sin = jnp.concatenate([jnp.sin(freqs)] * 2, -1)
            x1, x2 = (x[..., :D // 2], x[..., D // 2:])
            rotated = jnp.concatenate([-x2, x1], axis=-1)
            return x * cos[None, None] + rotated * sin[None, None]
        B, S, _ = hidden_states.shape

        def heads(x):
            return x.reshape(B, S, NUM_HEADS, HEAD_DIM).transpose(0, 2, 1, 3)
        q = heads(hidden_states @ Wq.T + bq)
        k = heads(hidden_states @ Wk.T + bk)
        v = heads(hidden_states @ Wv.T + bv)
        q = apply_rope(q)
        k = apply_rope(k)
        scores = jnp.einsum('bhqd,bhkd->bhqk', q, k) / jnp.sqrt(jnp.asarray(HEAD_DIM, q.dtype))
        causal = jnp.tril(jnp.ones((S, S), dtype=bool))
        scores = jnp.where(causal[None, None], scores, jnp.finfo(scores.dtype).min)
        weights = jax.nn.softmax(scores, axis=-1)
        context = jnp.einsum('bhqk,bhkd->bhqd', weights, v)
        merged = context.transpose(0, 2, 1, 3).reshape(B, S, INNER)
        return merged @ Wo.T + bo

    def _L0_ffn_ref(x, w1, w2, w3):
        import jax, jax.numpy as jnp
        import numpy as np
        EPS = 1e-08

        def _quantize(w):
            gamma = jnp.mean(jnp.abs(w))
            return jnp.clip(jnp.round(w / (gamma + EPS)), -1.0, 1.0)

        def _bitlinear(x, w):
            return jnp.matmul(x, _quantize(w).T)
        x1 = _bitlinear(x, w1)
        x2 = _bitlinear(x, w2)
        hidden = jax.nn.sigmoid(x1) * x2
        return _bitlinear(hidden, w3)

    def _L1_attn_ref(x, wq, wk, wv, wo):
        import jax, jax.numpy as jnp
        import numpy as np
        DIM = 256
        N_HEADS = 32
        N_KV_HEADS = 8
        HEAD_DIM = DIM // N_HEADS
        ROPE_BASE = 10000.0
        BATCH = 2
        SEQ = 256

        def _rope_cos_sin(seq_len, dtype=jnp.float32):
            inv_freq = 1.0 / ROPE_BASE ** (jnp.arange(0, HEAD_DIM, 2, dtype=jnp.float32) / HEAD_DIM)
            pos = jnp.arange(seq_len, dtype=jnp.float32)
            freqs = pos[:, None] * inv_freq[None, :]
            return (jnp.cos(freqs).astype(dtype), jnp.sin(freqs).astype(dtype))

        def _apply_rope(x, cos, sin):
            cos = cos[None, None, :, :]
            sin = sin[None, None, :, :]
            x_even = x[..., ::2]
            x_odd = x[..., 1::2]
            rot_even = x_even * cos - x_odd * sin
            rot_odd = x_even * sin + x_odd * cos
            out = jnp.stack((rot_even, rot_odd), axis=-1)
            return out.reshape(x.shape)
        b, s, _ = x.shape
        q = (x @ wq).reshape(b, s, N_HEADS, HEAD_DIM).transpose(0, 2, 1, 3)
        k = (x @ wk).reshape(b, s, N_KV_HEADS, HEAD_DIM).transpose(0, 2, 1, 3)
        v = (x @ wv).reshape(b, s, N_KV_HEADS, HEAD_DIM).transpose(0, 2, 1, 3)
        cos, sin = _rope_cos_sin(s, x.dtype)
        q = _apply_rope(q, cos, sin)
        k = _apply_rope(k, cos, sin)
        rep = N_HEADS // N_KV_HEADS
        if rep > 1:
            k = jnp.repeat(k, rep, axis=1)
            v = jnp.repeat(v, rep, axis=1)
        scores = jnp.einsum('bhqd,bhkd->bhqk', q, k) / HEAD_DIM ** 0.5
        causal = jnp.tril(jnp.ones((s, s), dtype=bool))
        scores = jnp.where(causal[None, None], scores, -jnp.inf)
        probs = jax.nn.softmax(scores, axis=-1)
        out = jnp.einsum('bhqk,bhkd->bhqd', probs, v)
        out = out.transpose(0, 2, 1, 3).reshape(b, s, DIM)
        return out @ wo

    def _L1_ffn_ref(x, w_gate, w_up, w_down):
        import jax, jax.numpy as jnp
        import numpy as np
        DIM_IN = 256
        DIM_HIDDEN = 1024
        gate = jnp.einsum('bsd,hd->bsh', x, w_gate)
        up = jnp.einsum('bsd,hd->bsh', x, w_up)
        gated = jax.nn.silu(gate) * up
        return jnp.einsum('bsh,dh->bsd', gated, w_down)
    x = L0_attn_hidden_states
    x = x + _layernorm(_L0_attn_ref(_layernorm(x, axis=-1), L0_attn_Wq, L0_attn_bq, L0_attn_Wk, L0_attn_bk, L0_attn_Wv, L0_attn_bv, L0_attn_Wo, L0_attn_bo), axis=-1)
    x = x + _layernorm(_L0_ffn_ref(_layernorm(x, axis=-1), L0_ffn_w1, L0_ffn_w2, L0_ffn_w3), axis=-1)
    x = x + _layernorm(_L1_attn_ref(_layernorm(x, axis=-1), L1_attn_wq, L1_attn_wk, L1_attn_wv, L1_attn_wo), axis=-1)
    x = x + _layernorm(_L1_ffn_ref(_layernorm(x, axis=-1), L1_ffn_w_gate, L1_ffn_w_up, L1_ffn_w_down), axis=-1)
    return x

_drawn_inputs = setup_inputs


def setup_inputs(seed=0):
    import zlib

    import numpy as np

    out = dict(_drawn_inputs(seed))
    spreads = {}
    factors = {'L0_attn_bq': 3.438, 'L0_attn_bk': 6.818, 'L1_attn_wq': 7.027, 'L1_attn_wk': 6.811}
    for name, (base, spread) in spreads.items():
        noise = np.random.default_rng([zlib.crc32(name.encode()), seed]).standard_normal(out[name].shape)
        drawn = base * np.exp(spread * noise) if base else spread * noise
        out[name] = jnp.asarray(drawn.astype(out[name].dtype))
    for name, factor in factors.items():
        out[name] = (out[name] * factor).astype(out[name].dtype)
    return out
```

```python
from contextlib import ExitStack

import concourse.bass as bass
from concourse import mybir

F32 = mybir.dt.float32
F16 = mybir.dt.float16
BF16 = mybir.dt.bfloat16
ALU = mybir.AluOpType
ACT = mybir.ActivationFunctionType
AX = mybir.AxisListType

P = 128
B, S, D = 2, 1024, 256
NT = B * S // P
TB = S // P
KT = D // P
BANK = 512
EPS = 1e-5
WSCALE = 64.0
MASKED = -1e30

H0, HD0 = 16, 128
F0 = 704
H1, G1, HD1 = 32, 8, 8
F1 = 1024


class Core:

    def __init__(self, nc, ctx):
        self.nc = nc
        self.ctx = ctx
        self.x = self.sb("x", [P, NT, D], F32)
        self.y = self.sb("y", [P, NT, D], F32)
        self.xT_hi = self.sb("xT_hi", [P, KT, B * S], F16)
        self.xT_lo = self.sb("xT_lo", [P, KT, B * S], F16)
        self.ident = self.sb("ident", [P, P], F32)
        self.ident_b = self.sb("ident_b", [P, P], BF16)
        self.ones_b = self.sb("ones_b", [P, P], BF16)
        self.ones = self.sb("ones", [P, P], F32)
        self.mask_kq = self.sb("mask_kq", [P, P], BF16)
        self.mask_qk = self.sb("mask_qk", [P, P], BF16)
        self.sems = []
        self.passed = nc.alloc_semaphore(name="passed")
        self.psum = ctx.enter_context(nc.psum_tensor("psum", [P, 8, BANK], F32))

    def sb(self, name, shape, dt, ctx=None):
        return (ctx or self.ctx).enter_context(self.nc.sbuf_tensor(name, shape, dt))

    def sem(self, name):
        self.sems.append(self.nc.alloc_semaphore(name=name))
        return self.sems[-1]

    def stand_alone(self, eng):
        eng.sem_inc(self.passed, 1)

    def end_phase(self):
        self.nc.all_engine_barrier()
        self.nc.clear_and_free_semaphores(self.sems)
        self.nc.all_engine_barrier()
        self.sems = []


def constants(c, x_in):
    nc = c.nc
    x_loaded, filled, selected = c.sem("x_loaded"), c.sem("filled"), c.sem("selected")
    with nc.Block() as block:
        @block.sync
        def _(sp):
            xv = x_in.rearrange("b (t p) d -> p (b t) d", p=P)
            for q in range(4):
                sp.dma_start(c.x[:, 4 * q:4 * q + 4, :], xv[:, 4 * q:4 * q + 4, :]).then_inc(x_loaded, 16)
            sp.wait_ge(x_loaded, 64)

        @block.gpsimd
        def _(pool):
            for buf, value in ((c.ident, 0.0), (c.ident_b, 0.0), (c.mask_kq, 0.0), (c.mask_qk, 0.0),
                               (c.ones_b, 1.0), (c.ones, 1.0)):
                pool.memset(buf[:, :], value).then_inc(filled, 1)
            pool.wait_ge(filled, 6)
            for buf in (c.ident, c.ident_b):
                pool.affine_select(out=buf[:, :], in_=buf[:, :], compare_op=ALU.not_equal, fill=1.0,
                                   base=0, pattern=[[-1, P]], channel_multiplier=1).then_inc(selected, 1)
            pool.affine_select(out=c.mask_kq[:, :], in_=c.mask_kq[:, :], compare_op=ALU.is_ge, fill=MASKED,
                               base=0, pattern=[[1, P]], channel_multiplier=-1).then_inc(selected, 1)
            pool.affine_select(out=c.mask_qk[:, :], in_=c.mask_qk[:, :], compare_op=ALU.is_ge, fill=MASKED,
                               base=0, pattern=[[-1, P]], channel_multiplier=1).then_inc(selected, 1)
            pool.wait_ge(selected, 4)


def boundary(c, name, add_y, make_xT, out=None):
    nc = c.nc
    PER = 4
    GRP = 2
    with ExitStack() as ctx:
        sb = lambda n, shape, dt=F32: c.sb(f"{name}_{n}", shape, dt, ctx)
        sem = lambda n: c.sem(f"{name}_{n}")
        stats = sb("stats", [P, NT, 6])
        msum, mdif, sq, m2, var, sd, inv, quo, avg, half, rstd, shift = (
            sb(n, [P, NT]) for n in ("msum", "mdif", "sq", "m2", "var", "sd", "inv", "quo", "avg", "half",
                                     "rstd", "shift"))
        xn = sb("xn", [P, PER, D])
        y_stats, x_stats, x_added = sem("y_stats"), sem("x_stats"), sem("x_added")
        step, var_ready, sd_ready, norm_ready = sem("step"), sem("var_ready"), sem("sd_ready"), sem("norm_ready")
        y_normed, xn_ready, turned, hi_ready, lo_ready = (
            sem("y_normed"), sem("xn_ready"), sem("turned"), sem("hi_ready"), sem("lo_ready"))
        stored = sem("stored")
        which = [w for w, on in (("y", add_y), ("x", make_xT)) if on]

        with nc.Block() as block:
            @block.vector
            def _(dve):
                steps = [0]

                def then_wait(ins):
                    steps[0] += 1
                    ins.then_inc(step, 1)
                    dve.wait_ge(step, steps[0])

                def normaliser(n):
                    then_wait(dve.tensor_tensor(msum[:, :], stats[:, :, 1], stats[:, :, 4], ALU.add))
                    then_wait(dve.tensor_tensor(mdif[:, :], stats[:, :, 1], stats[:, :, 4], ALU.subtract))
                    then_wait(dve.tensor_tensor(sq[:, :], mdif[:, :], mdif[:, :], ALU.mult))
                    then_wait(dve.tensor_tensor(m2[:, :], stats[:, :, 2], stats[:, :, 5], ALU.add))
                    then_wait(dve.tensor_scalar(m2[:, :], m2[:, :], 1.0 / D, EPS, ALU.mult, ALU.add))
                    dve.scalar_tensor_tensor(out=var[:, :], in0=sq[:, :], scalar=0.25, in1=m2[:, :],
                                             op0=ALU.mult, op1=ALU.add).then_inc(var_ready, 1)
                    dve.wait_ge(sd_ready, n)
                    dve.wait_ge(var_ready, n)
                    then_wait(dve.reciprocal(inv[:, :], sd[:, :]))
                    then_wait(dve.tensor_tensor(quo[:, :], var[:, :], inv[:, :], ALU.mult))
                    then_wait(dve.tensor_tensor(avg[:, :], quo[:, :], sd[:, :], ALU.add))
                    then_wait(dve.tensor_scalar(half[:, :], avg[:, :], 0.5, None, ALU.mult))
                    then_wait(dve.reciprocal(rstd[:, :], half[:, :]))
                    dve.scalar_tensor_tensor(out=shift[:, :], in0=msum[:, :], scalar=-0.5, in1=rstd[:, :],
                                             op0=ALU.mult, op1=ALU.mult).then_inc(norm_ready, 1)

                if add_y:
                    with dve.Fori(0, NT // PER) as i:
                        for j in range(PER):
                            dve.bn_stats(stats[:, bass.ds(i * PER + j, 1), :], c.y[:, bass.ds(i * PER + j, 1), :]).then_inc(y_stats, 1)
                    dve.wait_ge(y_stats, NT)
                    normaliser(1)
                    with dve.Fori(0, NT // PER) as i:
                        for j in range(PER):
                            t = i * PER + j
                            dve.wait_ge(y_normed, t + 1)
                            dve.tensor_tensor(c.x[:, bass.ds(t, 1), :], c.x[:, bass.ds(t, 1), :], c.y[:, bass.ds(t, 1), :],
                                              ALU.add).then_inc(x_added, 1)
                            if make_xT:
                                dve.wait_ge(x_added, t + 1)
                                c.stand_alone(dve)
                                dve.bn_stats(stats[:, bass.ds(t, 1), :], c.x[:, bass.ds(t, 1), :]).then_inc(x_stats, 1)
                elif make_xT:
                    with dve.Fori(0, NT // PER) as i:
                        for j in range(PER):
                            dve.bn_stats(stats[:, bass.ds(i * PER + j, 1), :], c.x[:, bass.ds(i * PER + j, 1), :]).then_inc(x_stats, 1)
                if make_xT:
                    dve.wait_ge(x_stats, NT)
                    normaliser(len(which))
                    with dve.Fori(0, NT // PER) as i:
                        for g in range(PER // GRP):
                            n = i * (PER // GRP) + g
                            dve.wait_ge(hi_ready, n + 1)
                            span = bass.ds(n * GRP * P, GRP * P)
                            dve.tensor_tensor(c.xT_lo[:, :, span],
                                              c.psum[:, g, :].rearrange("p (k n) -> p k n", k=KT),
                                              c.xT_hi[:, :, span], ALU.subtract).then_inc(lo_ready, 1)
                    dve.wait_ge(lo_ready, NT // GRP)

            @block.scalar
            def _(act):
                for n, w in enumerate(which):
                    act.wait_ge(var_ready, n + 1)
                    act.activation(sd[:, :], var[:, :], ACT.Sqrt).then_inc(sd_ready, 1)
                    act.wait_ge(norm_ready, n + 1)
                    if w == "y":
                        with act.Fori(0, NT // PER) as i:
                            for j in range(PER):
                                t = i * PER + j
                                act.activation(c.y[:, bass.ds(t, 1), :], c.y[:, bass.ds(t, 1), :], ACT.Identity,
                                               bias=shift[:, bass.ds(t, 1)],
                                               scale=rstd[:, bass.ds(t, 1)]).then_inc(y_normed, 1)
                    else:
                        with act.Fori(0, NT // PER) as i:
                            for g in range(PER // GRP):
                                m = i * (PER // GRP) + g
                                for j in range(g * GRP, g * GRP + GRP):
                                    t = i * PER + j
                                    act.activation(xn[:, j, :], c.x[:, bass.ds(t, 1), :], ACT.Identity,
                                                   bias=shift[:, bass.ds(t, 1)],
                                                   scale=rstd[:, bass.ds(t, 1)]).then_inc(xn_ready, 1)
                                act.wait_ge(turned, m + 1)
                                c.stand_alone(act)
                                act.activation(c.xT_hi[:, :, bass.ds(m * GRP * P, GRP * P)],
                                               c.psum[:, g, :].rearrange("p (k n) -> p k n", k=KT),
                                               ACT.Copy).then_inc(hi_ready, 1)
                                act.wait_ge(lo_ready, m + 1)
                                c.stand_alone(act)

            if make_xT:
                @block.tensor
                def _(pe):
                    with pe.Fori(0, NT // PER) as i:
                        for g in range(PER // GRP):
                            pe.wait_ge(xn_ready, i * PER + g * GRP + GRP)
                            for j in range(GRP):
                                for k in range(KT):
                                    last = pe.transpose(c.psum[:, g, k * GRP * P + j * P:k * GRP * P + (j + 1) * P],
                                                        xn[:, g * GRP + j, k * P:(k + 1) * P], c.ident[:, :])
                            last.then_inc(turned, 1)

            if out is not None:
                @block.sync
                def _(sp):
                    ov = out.rearrange("b (t p) d -> p (b t) d", p=P)
                    for q in range(NT // PER):
                        sp.wait_ge(x_added, PER * (q + 1))
                        sp.dma_start(ov[:, PER * q:PER * q + PER, :], c.x[:, PER * q:PER * q + PER, :]).then_inc(stored, 16)
                    sp.wait_ge(stored, 16 * (NT // PER))


def program(nc, ins, out):
    with ExitStack() as ctx:
        c = Core(nc, ctx)
        constants(c, ins["L0_attn_hidden_states"])
        boundary(c, "in", False, True)
        attention_0(c, ins)
        c.end_phase()
        boundary(c, "mid1", True, True)
        ffn_0(c, ins)
        c.end_phase()
        boundary(c, "mid2", True, True)
        attention_1(c, ins)
        c.end_phase()
        boundary(c, "mid3", True, True)
        ffn_1(c, ins)
        boundary(c, "end", True, False, out)


def wait(eng, sem, value):
    if not (isinstance(value, int) and value <= 0):
        eng.wait_ge(sem, value)


def spans(lo, hi):
    while lo < hi:
        end = min(hi, (lo // BANK + 1) * BANK)
        yield lo, end
        lo = end


def attention_0(c, ins):
    nc = c.nc
    SCALE = float(HD0) ** -0.5
    CH = S // BANK
    NP = 4
    inner = H0 * HD0
    w_in = [ins[f"L0_attn_W{n}"].rearrange("(k p) o -> p k o", p=P) for n in "qkv"]
    wo_in = ins["L0_attn_Wo"]

    PREP = [("proj", 0, 0), ("proj", 0, 1), ("proj", 1, 0), ("proj", 1, 1)]
    VALS = [("vals", 0), ("vals", 1)]
    SUMS = [("sums",)]
    OUTS = [("out", i) for i in range(TB // 2)]
    SCAN = [("scan", (0, 0), (1, 0))] + [("scan", (t, n)) for t in range(2, TB) for n in range((t * P) // BANK + 1)]
    ITEMS = [PREP, VALS, SCAN[0:2], SUMS + SCAN[2:4], OUTS[0:1] + SCAN[4:6], OUTS[1:2] + SCAN[6:8],
             OUTS[2:3] + SCAN[8:10], OUTS[3:4] + SCAN[10:11]]
    FIRST = PREP + VALS + SCAN
    no_out = [[i for i in s if i[0] not in ("sums", "out")] for s in ITEMS]
    only_out = [[i for i in s if i[0] in ("sums", "out")] for s in ITEMS]
    count = lambda steps: sum(map(len, steps))
    N_FIRST = len(FIRST) + count(no_out) + count(ITEMS)
    N_HEAD = 2 * count(ITEMS)
    assert N_FIRST % 2 == 0 and count(ITEMS) % 2 == 0

    with ExitStack() as ctx:
        sb = lambda n, shape, dt=F32: c.sb(f"a0_{n}", shape, dt, ctx)
        sem = lambda n: c.sem(f"a0_{n}")
        cos, sin = sb("cos", [P, S]), sb("sin", [P, S])
        w_raw = sb("w_raw", [P, 3, KT, P])
        w_hi, w_lo = sb("w_hi", [P, 3, KT, P], F16), sb("w_lo", [P, 3, KT, P], F16)
        woT = sb("woT", [P, D])
        bias, head_bias = sb("bias", [P, 2, H0]), sb("head_bias", [P, 2])
        bias_v = sb("bias_v", [P, inner])
        lin, rot, cosd, rope = (sb(n, [P, 2, BANK]) for n in ("lin", "rot", "cosd", "rope"))
        hi = {0: sb("q_hi", [P, 2, S], F16), 1: sb("k_hi", [P, 2, S], F16)}
        lo = {0: sb("q_lo", [P, 2, S], F16), 1: sb("k_lo", [P, 2, S], F16)}
        val = sb("val", [P, 2, TB, HD0])
        mx, mx_all = sb("mx", [P, 2, TB, 2]), sb("mx_all", [P, 2, TB])
        diag = sb("diag", [P, 2, S], BF16)
        prob = sb("prob", [P, NP, S])
        psumk = sb("psumk", [P, 2, S])
        psumk_hi, psumk_lo = sb("psumk_hi", [P, S], F16), sb("psumk_lo", [P, S], F16)
        ctxT = sb("ctxT", [P, 2, S])
        rsum = sb("rsum", [P, 2, TB])

        tables, w_loaded, wo_loaded, bias_loaded = sem("tables"), sem("w_loaded"), sem("wo_loaded"), sem("bias_loaded")
        w_used, bias_ready = sem("w_used"), sem("bias_ready")
        biasv_loaded, y_started = sem("biasv_loaded"), sem("y_started")
        work_ready, work_free = [sem(f"work_ready{i}") for i in range(2)], [sem(f"work_free{i}") for i in range(2)]
        whi_ready, wlo_ready = sem("whi_ready"), sem("wlo_ready")
        sums_hi, sums_lo = sem("sums_hi"), sem("sums_lo")
        lin_ready, cosd_ready, rot_ready, rope_ready = sem("lin_ready"), sem("cosd_ready"), sem("rot_ready"), sem("rope_ready")
        rhi_ready, qk_ready, v_ready = sem("rhi_ready"), sem("qk_ready"), sem("v_ready")
        mx_ready, diag_ready = sem("mx_ready"), sem("diag_ready")
        scores_ready, prob_ready, context_done, summed = sem("scores_ready"), sem("prob_ready"), sem("context_done"), sem("summed")
        ctxT_ready, rsum_ready, out_done, y_added = sem("ctxT_ready"), sem("rsum_ready"), sem("out_done"), sem("y_added")

        def work(slot, a, b):
            return c.psum[:, 6 + slot, a:b]

        def scores(kt, a, b):
            bank = 2 * (kt % 2) + a // BANK
            return c.psum[:, bank, a % BANK:a % BANK + b - a]

        def scores_row(kt, a):
            pair = c.psum[:, 2 * (kt % 2):2 * (kt % 2) + 2, :].rearrange("p b n -> p (b n)")
            return pair[:, a:S]

        def context(a, b):
            return c.psum[:, 4 + a // BANK, a % BANK:a % BANK + b - a]

        def run(eng, do_item, step_begin, step_end, weights=None, unit_end=None, before_item=None):
            def unit(h, b, number, steps, next_unit):
                for kt in range(TB):
                    step_begin(2 * h + b, b, kt)
                    for n, item in enumerate(steps[kt]):
                        if before_item:
                            before_item(2 * h + b, b, kt, n, len(steps[kt]))
                        do_item(item, number, h, b, next_unit)
                        number = (number[0], number[1] + 1)
                    if before_item:
                        before_item(2 * h + b, b, kt, len(steps[kt]), len(steps[kt]))
                    step_end(2 * h + b, b, kt)
                    if weights and b == 0 and kt == 4 and not (isinstance(h, int) and h == H0 - 1):
                        weights(h)
                if unit_end:
                    unit_end(h, b)
                return number

            number = (0, 0)
            if weights:
                weights(-1)
            for item in FIRST:
                do_item(item, number, -1, 1, 0)
                number = (0, number[1] + 1)
            number = unit(0, 0, number, no_out, 1)
            number = unit(0, 1, number, ITEMS, 2)
            assert number[1] == N_FIRST
            with eng.Fori(1, H0 - 1) as h:
                number = ((h - 1) * (N_HEAD // 2) + N_FIRST // 2, 0)
                number = unit(h, 0, number, ITEMS, 2 * h + 1)
                unit(h, 1, number, ITEMS, 2 * h + 2)
            number = ((H0 - 2) * (N_HEAD // 2) + N_FIRST // 2, 0)
            number = unit(H0 - 1, 0, number, ITEMS, 2 * H0 - 1)
            number = unit(H0 - 1, 1, number, only_out, None)
            for item in SUMS + OUTS:
                do_item(item, number, H0, 0, None)
                number = (number[0], number[1] + 1)

        def column(index, n=1):
            return slice(index * n, index * n + n) if isinstance(index, int) else bass.ds(index * n, n)

        def turn(number):
            return number[1] % 2, number[0] + number[1] // 2

        with nc.Block() as block:
            @block.sync
            def _(sp):
                sp.dma_start(cos[:, :], ins["rope0_cos"]).then_inc(tables, 16)
                sp.dma_start(sin[:, :], ins["rope0_sin"]).then_inc(tables, 16)

                def load_head(h, at):
                    wait(sp, w_used, h)
                    for j in range(3):
                        sp.dma_start(w_raw[:, j, :, :], w_in[j][:, :, at]).then_inc(w_loaded, 16)

                load_head(0, slice(0, P))
                for j, n in enumerate("qk"):
                    sp.dma_start(bias[:, j, :], ins[f"L0_attn_b{n}"]).then_inc(bias_loaded, 16)
                sp.dma_start(bias_v[:, :], ins["L0_attn_bv"].rearrange("(a i) -> a i", a=1).broadcast_to([P, inner])).then_inc(biasv_loaded, 16)
                sp.dma_start(woT[:, :], wo_in[0:P, :]).then_inc(wo_loaded, 16)
                sp.dma_start(c.y[:, :, :], ins["L0_attn_bo"].rearrange("(a t i) -> a t i", a=1, t=1).broadcast_to([P, NT, D])).then_inc(y_started, 16)
                with sp.Fori(1, H0) as h:
                    load_head(h, bass.ds(sp.snap(h * P), P))

            @block.tensor
            def _(pe):
                def do_item(item, number, h, b, w):
                    slot, before = turn(number)
                    wait(pe, work_free[slot], before)
                    kind = item[0]
                    if kind == "proj":
                        _, j, ch = item
                        wb = 1 - b
                        pe.wait_ge(wlo_ready, (h + 1 if b else h) * 3 + 1 + j)
                        tok = slice(wb * S + ch * BANK, wb * S + (ch + 1) * BANK)
                        terms = [(w_hi, c.xT_hi), (w_hi, c.xT_lo), (w_lo, c.xT_hi)]
                        for n, (a, m, k) in enumerate([(a, m, k) for k in range(KT) for a, m in terms]):
                            last = pe.matmul(work(slot, 0, BANK), a[:, j, k, :], m[:, k, tok],
                                             start=(n == 0), stop=(n == 3 * KT - 1))
                    elif kind == "vals":
                        wb = 1 - b
                        pe.wait_ge(wlo_ready, (h + 1 if b else h) * 3 + 3)
                        for t in range(4):
                            tok = slice(wb * S + (item[1] * 4 + t) * P, wb * S + (item[1] * 4 + t + 1) * P)
                            n = 0
                            for k in range(KT):
                                for m, a in ((c.xT_hi, w_hi), (c.xT_hi, w_lo), (c.xT_lo, w_hi)):
                                    last = pe.matmul(work(slot, t * P, (t + 1) * P), m[:, k, tok], a[:, 2, k, :],
                                                     start=(n == 0), stop=(n == 3 * KT - 1))
                                    n += 1
                    elif kind == "scan":
                        wb = 1 - b
                        pe.wait_ge(qk_ready, w * 4 + 4)
                        col = 0
                        for t, part in item[1:]:
                            a, e = part * BANK, min((part + 1) * BANK, (t + 1) * P)
                            edge = e == (t + 1) * P
                            last = pe.matmul(work(slot, col, col + e - a), hi[0][:, wb, t * P:(t + 1) * P],
                                             hi[1][:, wb, a:e], start=True, stop=not edge)
                            col += e - a
                            if edge:
                                last = pe.matmul(work(slot, col - P, col), c.ident_b[:, :], c.mask_qk[:, :],
                                                 start=False, stop=True)
                    elif kind == "sums":
                        pu, pb = 2 * h + b - 1, 1 - b
                        pe.wait_ge(sums_lo, pu + 1)
                        for t in range(TB):
                            for n, part in enumerate((psumk_hi, psumk_lo)):
                                last = pe.matmul(work(slot, t, t + 1), part[:, t * P:(t + 1) * P], c.ones_b[:, 0:1],
                                                 start=(n == 0), stop=(n == 1))
                    elif kind == "out":
                        pu, pb = 2 * h + b - 1, 1 - b
                        pe.wait_ge(ctxT_ready, pu + 1)
                        pe.wait_ge(wo_loaded, 16 * (h if b == 0 else h + 1))
                        for t in range(2):
                            tt = item[1] * 2 + t
                            last = pe.matmul(work(slot, t * D, (t + 1) * D), ctxT[:, pb, tt * P:(tt + 1) * P], woT[:, :],
                                             start=True, stop=True)
                    last.then_inc(work_ready[slot], 1)

                def make_scores(u, b, kt):
                    if kt == 0:
                        pe.wait_ge(diag_ready, u * TB + TB)
                    wait(pe, prob_ready, u * TB + kt - 1)
                    keys = slice(kt * P, (kt + 1) * P)
                    pieces = list(spans(kt * P, S))
                    for n, (a, e) in enumerate(pieces):
                        terms = [(hi[1][:, b, keys], hi[0]), (hi[1][:, b, keys], lo[0]), (lo[1][:, b, keys], hi[0])]
                        for m, (kk, qq) in enumerate(terms):
                            pe.matmul(scores(kt, a, e), kk, qq[:, b, a:e], start=(m == 0), stop=False)
                        if n == 0:
                            pe.matmul(scores(kt, a, a + P), c.ident_b[:, :], c.mask_kq[:, :], start=False, stop=False)
                        last = pe.matmul(scores(kt, a, e), c.ones_b[:, :], diag[:, b, a:e], start=False, stop=True)
                    last.then_inc(scores_ready, 1)

                def before_item(u, b, kt, i, n):
                    first = min(1, n)
                    if kt == 0 and i == first:
                        make_scores(u, b, 0)
                    if kt + 1 < TB and i == (min(2, n) if kt == 0 else first):
                        make_scores(u, b, kt + 1)
                    if i == (n if kt == 0 or n < 3 else n - 1):
                        make_context(u, b, kt)

                def make_context(u, b, kt):
                    pe.wait_ge(prob_ready, u * TB + kt + 1)
                    if kt == 0:
                        wait(pe, ctxT_ready, u)
                    for a, e in spans(kt * P, S):
                        last = pe.matmul(context(a, e), val[:, b, kt, :], prob[:, kt % NP, a:e],
                                         start=(kt == 0), stop=(kt == (min(e, S) - 1) // P))
                    last.then_inc(context_done, 1)

                run(pe, do_item, lambda *a: None, lambda *a: None, before_item=before_item)

            @block.scalar
            def _(act):
                def do_item(item, number, h, b, w):
                    slot, before = turn(number)
                    kind = item[0]
                    if kind == "proj":
                        _, j, ch = item
                        n = w * 4 + 2 * j + ch
                        act.wait_ge(work_ready[slot], before + 1)
                        wait(act, qk_ready, n - 1)
                        if j == 0 and ch == 0:
                            act.wait_ge(bias_ready, (h + 1 if b else h) + 1)
                        act.activation(lin[:, ch, :], work(slot, 0, BANK), ACT.Identity, bias=head_bias[:, j:j + 1],
                                       scale=1.0 / WSCALE).then_inc(lin_ready, 1)

                def weights(h):
                    act.wait_ge(w_loaded, (h + 1) * 48 + 48)
                    wait(act, v_ready, (h + 1) * 4)
                    for j in range(3):
                        act.activation(w_hi[:, j, :, :], w_raw[:, j, :, :], ACT.Copy, scale=WSCALE).then_inc(whi_ready, 1)

                def step_begin(u, b, kt):
                    act.wait_ge(scores_ready, u * TB + kt + 1)
                    wait(act, context_done, u * TB + kt - NP + 1)
                    wait(act, summed, u * TB + kt - NP + (2 if kt == NP else 1))
                    act.activation(prob[:, kt % NP, kt * P:S], scores_row(kt, kt * P), ACT.Exp,
                                   scale=SCALE).then_inc(prob_ready, 1)

                def split_sums(pu, pb):
                    act.wait_ge(summed, pu * TB + TB)
                    wait(act, rsum_ready, pu)
                    act.activation(psumk_hi[:, :], psumk[:, pb, :], ACT.Copy).then_inc(sums_hi, 1)

                def step_end(u, b, kt):
                    if kt == 0 and not (isinstance(u, int) and u == 0):
                        split_sums(u - 1, 1 - b)

                def unit_end(h, b):
                    u = 2 * h + b
                    act.wait_ge(context_done, u * TB + TB)
                    wait(act, out_done, u - 1)
                    act.activation(ctxT[:, b, :], c.psum[:, 4:6, :].rearrange("p b n -> p (b n)"),
                                   ACT.Copy).then_inc(ctxT_ready, 1)
                    if b == 0 and not (isinstance(h, int) and h == 0):
                        act.wait_ge(out_done, u)
                        act.dma_start(woT[:, :], wo_in[column(h, P), :]).then_inc(wo_loaded, 16)

                run(act, do_item, step_begin, step_end, weights, unit_end)
                split_sums(2 * H0 - 1, 1)

            @block.vector
            def _(dve):
                dve.wait_ge(tables, 32)
                dve.wait_ge(y_started, 16)
                dve.wait_ge(biasv_loaded, 16)
                dve.wait_ge(bias_loaded, 32)

                def do_item(item, number, h, b, w):
                    slot, before = turn(number)
                    kind = item[0]
                    wb = 1 - b
                    if kind == "proj":
                        _, j, ch = item
                        n = w * 4 + 2 * j + ch
                        tok = slice(ch * BANK, (ch + 1) * BANK)
                        dve.wait_ge(lin_ready, n + 1)
                        dve.sem_inc(work_free[slot], 1)
                        wait(dve, qk_ready, n - 1)
                        dve.tensor_tensor(rot[0:64, ch, :], lin[64:128, ch, :], sin[64:128, tok], ALU.mult).then_inc(rot_ready, 1)
                        dve.tensor_tensor(rot[64:128, ch, :], lin[0:64, ch, :], sin[0:64, tok], ALU.mult).then_inc(rot_ready, 1)
                        dve.wait_ge(rot_ready, n * 2 + 2)
                        dve.wait_ge(cosd_ready, n + 1)
                        dve.tensor_tensor(rope[:, ch, :], rot[:, ch, :], cosd[:, ch, :], ALU.add).then_inc(rope_ready, 1)
                        dve.wait_ge(rope_ready, n + 1)
                        if j == 0 and ch == 0:
                            wait(dve, scores_ready, w * TB - TB)
                        dve.tensor_copy(hi[j][:, wb, tok], rope[:, ch, :]).then_inc(rhi_ready, 1)
                        dve.wait_ge(rhi_ready, n + 1)
                        dve.tensor_tensor(lo[j][:, wb, tok], rope[:, ch, :], hi[j][:, wb, tok], ALU.subtract).then_inc(qk_ready, 1)
                    elif kind == "vals":
                        i = item[1]
                        dve.wait_ge(work_ready[slot], before + 1)
                        if i == 0:
                            wait(dve, context_done, w * TB - TB)
                        dve.scalar_tensor_tensor(out=val[:, wb, 4 * i:4 * i + 4, :],
                                                 in0=work(slot, 0, BANK).rearrange("p (t n) -> p t n", t=4),
                                                 scalar=1.0 / WSCALE,
                                                 in1=bias_v[:, column(h + 1 if b else h, HD0)].unsqueeze(1).broadcast_to([P, 4, HD0]),
                                                 op0=ALU.mult, op1=ALU.add).then_inc(v_ready, 1)
                        dve.wait_ge(v_ready, w * 2 + i + 1)
                        dve.sem_inc(work_free[slot], 1)
                    elif kind == "scan":
                        dve.wait_ge(work_ready[slot], before + 1)
                        col = 0
                        for t, part in item[1:]:
                            n = min(BANK, (t + 1) * P - part * BANK)
                            ins = dve.tensor_reduce(mx[:, wb, t, part:part + 1], work(slot, col, col + n), AX.X, ALU.max)
                            col += n
                            ins.then_inc(mx_ready, 1)
                        t, part = item[-1]
                        n = w * 16 + (t if t < 4 else 4 + 3 * (t - 4)) + part + 1
                        dve.wait_ge(mx_ready, n)
                        dve.sem_inc(work_free[slot], 1)
                        for t, part in item[1:]:
                            two = t * P >= BANK
                            if two and part == 0:
                                continue
                            top = mx[:, wb, t, 0:1]
                            if two:
                                top = mx_all[:, wb, t:t + 1]
                                dve.tensor_tensor(top, mx[:, wb, t, 0:1], mx[:, wb, t, 1:2], ALU.max).then_inc(mx_ready, 1)
                                dve.wait_ge(mx_ready, n + 1)
                            if t == 0:
                                wait(dve, scores_ready, w * TB - TB)
                            dve.tensor_scalar(diag[:, wb, t * P:(t + 1) * P], c.ident_b[:, :], top, -1.0,
                                              ALU.mult, ALU.mult).then_inc(diag_ready, 1)
                    elif kind == "sums":
                        pu, pb = 2 * h + b - 1, 1 - b
                        dve.wait_ge(work_ready[slot], before + 1)
                        dve.reciprocal(rsum[:, pb, :], work(slot, 0, TB)).then_inc(rsum_ready, 1)
                        dve.wait_ge(rsum_ready, pu + 1)
                        dve.sem_inc(work_free[slot], 1)
                    elif kind == "out":
                        pu, pb = 2 * h + b - 1, 1 - b
                        dve.wait_ge(work_ready[slot], before + 1)
                        if item[1] == 0:
                            wait(dve, y_added, pu * TB - TB)
                        for t in range(2):
                            tt = item[1] * 2 + t
                            yt = c.y[:, pb * TB + tt, :]
                            dve.scalar_tensor_tensor(out=yt, in0=work(slot, t * D, (t + 1) * D), scalar=rsum[:, pb, tt:tt + 1],
                                                     in1=yt, op0=ALU.mult, op1=ALU.add).then_inc(y_added, 1)
                        dve.wait_ge(y_added, pu * TB + item[1] * 2 + 2)
                        dve.sem_inc(work_free[slot], 1)
                        if item[1] == TB // 2 - 1:
                            dve.sem_inc(out_done, 1)

                def weights(h):
                    for j in range(3):
                        dve.wait_ge(whi_ready, (h + 1) * 3 + j + 1)
                        dve.scalar_tensor_tensor(out=w_lo[:, j, :, :], in0=w_raw[:, j, :, :], scalar=WSCALE, in1=w_hi[:, j, :, :],
                                                 op0=ALU.mult, op1=ALU.subtract).then_inc(wlo_ready, 1)
                    wait(dve, lin_ready, (h + 1) * 8)
                    dve.tensor_scalar(head_bias[:, :], bias[:, :, column(h + 1)], 1.0, None, ALU.mult).then_inc(bias_ready, 1)
                    dve.wait_ge(wlo_ready, (h + 1) * 3 + 3)
                    dve.sem_inc(w_used, 1)

                run(dve, do_item, lambda *a: None, lambda *a: None, weights)

            @block.gpsimd
            def _(pool):
                pool.wait_ge(tables, 32)

                def do_item(item, number, h, b, w):
                    if item[0] == "proj":
                        _, j, ch = item
                        n = w * 4 + 2 * j + ch
                        pool.wait_ge(lin_ready, n + 1)
                        wait(pool, rope_ready, n - 1)
                        pool.tensor_tensor(cosd[:, ch, :], lin[:, ch, :], cos[:, ch * BANK:(ch + 1) * BANK],
                                           ALU.mult).then_inc(cosd_ready, 1)

                def split_sums(pu, pb):
                    pool.wait_ge(sums_hi, pu + 1)
                    pool.tensor_tensor(psumk_lo[:, :], psumk[:, pb, :], psumk_hi[:, :], ALU.subtract).then_inc(sums_lo, 1)

                def step_end(u, b, kt):
                    if kt == 0 and not (isinstance(u, int) and u == 0):
                        split_sums(u - 1, 1 - b)
                    pool.wait_ge(prob_ready, u * TB + kt + 1)
                    if kt == 0:
                        wait(pool, out_done, u - 1)
                        pool.tensor_tensor(psumk[:, b, 0:P], prob[:, 0, 0:P], c.ones[:, :], ALU.mult).then_inc(summed, 1)
                    elif kt == 1:
                        pool.tensor_tensor(psumk[:, b, P:S], prob[:, 0, P:S], prob[:, 1, P:S], ALU.add).then_inc(summed, 1)
                    else:
                        pool.wait_ge(summed, u * TB + kt)
                        pool.tensor_tensor(psumk[:, b, kt * P:S], psumk[:, b, kt * P:S], prob[:, kt % NP, kt * P:S],
                                           ALU.add).then_inc(summed, 1)

                run(pool, do_item, lambda *a: None, step_end)
                split_sums(2 * H0 - 1, 1)


def ffn(c, name, width, ins_w, quantised):
    nc = c.nc
    HT = -(-width // P)
    FULL, REST = width // P, width % P
    CH = B * S // BANK
    TC = BANK // P
    WP = 1 if quantised else 2
    UNSCALE = 1.0 if quantised else 1.0 / WSCALE
    TERMS = [(wi, xi) for wi in range(WP) for xi in range(2) if wi + xi <= 1]
    W_EPS = 1e-8

    with ExitStack() as ctx:
        sb = lambda n, shape, dt=F32: c.sb(f"{name}_{n}", shape, dt, ctx)
        sem = lambda n: c.sem(f"{name}_{n}")
        wT = [[sb(f"w{j}T{i}", [P, KT, HT * P] if j < 2 else [P, HT, D], F16) for i in range(WP)] for j in range(3)]
        work_ready, work_free, part_ready = [sem(f"work_ready{i}") for i in range(4)], [sem(f"work_free{i}") for i in range(4)], sem("part_ready")

        def weights():
            with ExitStack() as wctx:
                raw = [c.sb(f"{name}_raw{j}", [P, HT, D] if j < 2 else [P, KT, HT * P], F32, wctx) for j in range(3)]
                flat = [r[:, :, :].rearrange("p a b -> p (a b)") for r in raw]
                padded, loaded = sem("padded"), [sem(f"loaded{j}") for j in range(3)]
                mag, total = c.sb(f"{name}_mag", [P, 3], F32, wctx), c.psum[:, 7, 0:3]
                scrap = c.sb(f"{name}_scrap", [P, HT * D], F32, wctx)
                gam, pos, neg = (c.sb(f"{name}_{n}", [P, 3], F32, wctx) for n in ("gam", "pos", "neg"))
                mag_ready, total_ready, thr = sem("mag_ready"), sem("total_ready"), sem("thr")
                neg_ready, q_ready = sem("neg_ready"), sem("q_ready")
                items = [(j, ht) for j in range(3) for ht in range(HT)]

                with nc.Block() as block:
                    @block.sync
                    def _(sp):
                        if REST:
                            sp.wait_ge(padded, 3)
                        for j in range(3):
                            if j < 2:
                                sp.dma_start(raw[j][:, 0:FULL, :], ins_w[j][0:FULL * P, :].rearrange("(a p) d -> p a d", p=P)).then_inc(loaded[j], 16)
                                if REST:
                                    sp.dma_start(raw[j][0:REST, FULL, :], ins_w[j][FULL * P:width, :]).then_inc(loaded[j], 16)
                            else:
                                sp.dma_start(raw[j][:, :, 0:width], ins_w[j].rearrange("(a p) h -> p a h", p=P)).then_inc(loaded[j], 16)

                    def arrived(eng, j):
                        eng.wait_ge(loaded[j], 32 if REST and j < 2 else 16)

                    @block.gpsimd
                    def _(pool):
                        if REST:
                            for j in range(3):
                                pad = raw[j][:, FULL, :] if j < 2 else raw[j][:, :, width:HT * P]
                                pool.memset(pad, 0.0).then_inc(padded, 1)

                    @block.tensor
                    def _(pe):
                        if quantised:
                            pe.wait_ge(mag_ready, 3)
                            pe.matmul(total, c.ones[:, :], mag[:, :], start=True, stop=True).then_inc(total_ready, 1)
                        for n, (j, ht) in enumerate(items):
                            if ht == 0:
                                pe.wait_ge(q_ready, j + 1) if quantised else arrived(pe, j)
                            wait(pe, work_free[n % 4], n // 4)
                            for k in range(KT):
                                block_in = raw[j][:, ht, k * P:(k + 1) * P] if j < 2 else raw[j][:, k, ht * P:(ht + 1) * P]
                                last = pe.transpose(c.psum[:, n % 4, k * P:(k + 1) * P], block_in, c.ident[:, :])
                            last.then_inc(work_ready[n % 4], 1)

                    def parts(n):
                        j, ht = items[n]
                        src = c.psum[:, n % 4, 0:D]
                        if j < 2:
                            return src.rearrange("p (k n) -> p k n", k=KT), [w[:, :, ht * P:(ht + 1) * P] for w in wT[j]]
                        return src, [w[:, ht, :] for w in wT[j]]

                    @block.scalar
                    def _(act):
                        if quantised:
                            for j in range(3):
                                arrived(act, j)
                                wait(act, mag_ready, j)
                                act.activation(scrap[:, :], flat[j], ACT.Abs, accum_out=mag[:, j:j + 1]).then_inc(mag_ready, 1)
                        for n in range(len(items)):
                            src, dst = parts(n)
                            act.wait_ge(work_ready[n % 4], n // 4 + 1)
                            ins = act.activation(dst[0], src, ACT.Copy, scale=1.0 if quantised else WSCALE)
                            ins.then_inc(work_free[n % 4] if quantised else part_ready, 1)

                    @block.vector
                    def _(dve):
                        if quantised:
                            dve.wait_ge(total_ready, 1)
                            dve.tensor_scalar(gam[:, :], total, 1.0 / (width * D), W_EPS, ALU.mult, ALU.add).then_inc(thr, 1)
                            dve.wait_ge(thr, 1)
                            dve.tensor_scalar(pos[:, :], gam[:, :], 0.5, None, ALU.mult).then_inc(thr, 1)
                            dve.tensor_scalar(neg[:, :], gam[:, :], -0.5, None, ALU.mult).then_inc(thr, 1)
                            dve.wait_ge(thr, 3)
                            for j in range(3):
                                wait(dve, q_ready, j)
                                dve.tensor_scalar(scrap[:, :], flat[j], neg[:, j:j + 1], -1.0, ALU.is_lt, ALU.mult).then_inc(neg_ready, 1)
                                dve.wait_ge(neg_ready, j + 1)
                                dve.scalar_tensor_tensor(out=flat[j], in0=flat[j], scalar=pos[:, j:j + 1], in1=scrap[:, :],
                                                         op0=ALU.is_gt, op1=ALU.add).then_inc(q_ready, 1)
                        else:
                            for n in range(len(items)):
                                src, dst = parts(n)
                                dve.wait_ge(part_ready, n + 1)
                                dve.scalar_tensor_tensor(out=dst[1], in0=src, scalar=WSCALE, in1=dst[0], op0=ALU.mult,
                                                         op1=ALU.subtract).then_inc(work_free[n % 4], 1)

        weights()

        sig, gate = sb("sig", [P, 2, BANK]), sb("gate", [P, 2, BANK])
        hid = sb("hid", [P, 2, BANK])
        hidT = [sb(f"hidT{i}", [P, HT, BANK], F16) for i in range(2)]
        gate_made, up_made, sig_ready, gate_ready, hid_ready, hid_hi, hid_lo = (
            sem(n) for n in ("gate_made", "up_made", "sig_ready", "gate_ready", "hid_ready", "hid_hi", "hid_lo"))
        down_made, y_ready = sem("down_made"), sem("y_ready")

        def hidden(j, ht):
            return c.psum[:, 2 * j + ht % 2, :]

        with nc.Block() as block:
            @block.tensor
            def _(pe):
                with pe.Fori(0, CH) as ch:
                    tok = bass.ds(ch * BANK, BANK)
                    for ht in range(HT):
                        for j in range(2):
                            if ht >= 2:
                                pe.wait_ge(hid_ready, ch * HT + ht - 1)
                            for n, (k, wi, xi) in enumerate([(k, wi, xi) for k in range(KT) for wi, xi in TERMS]):
                                last = pe.matmul(hidden(j, ht), wT[j][wi][:, k, ht * P:(ht + 1) * P],
                                                 (c.xT_hi, c.xT_lo)[xi][:, k, tok],
                                                 start=(n == 0), stop=(n == KT * len(TERMS) - 1))
                            last.then_inc((gate_made, up_made)[j], 1)
                    pe.wait_ge(hid_lo, ch * HT + HT)
                    for t in range(TC):
                        for n, (ht, wi, xi) in enumerate([(ht, wi, xi) for ht in range(HT) for wi, xi in TERMS]):
                            last = pe.matmul(c.psum[:, 4 + t, 0:D], hidT[xi][:, ht, t * P:(t + 1) * P], wT[2][wi][:, ht, :],
                                             start=(n == 0), stop=(n == HT * len(TERMS) - 1))
                        last.then_inc(down_made, 1)
                    pe.wait_ge(y_ready, ch * TC + TC)

            @block.scalar
            def _(act):
                with act.Fori(0, CH) as ch:
                    for ht in range(HT + 1):
                        if ht < HT:
                            n = ch * HT + ht
                            act.wait_ge(gate_made, n + 1)
                            if ht >= 2:
                                act.wait_ge(hid_ready, n - 1)
                            act.activation(sig[:, ht % 2, :], hidden(0, ht), ACT.Sigmoid, scale=UNSCALE).then_inc(sig_ready, 1)
                        if ht >= 1:
                            n = ch * HT + ht - 1
                            act.wait_ge(hid_ready, n + 1)
                            act.activation(hidT[0][:, ht - 1, :], hid[:, (ht - 1) % 2, :], ACT.Copy).then_inc(hid_hi, 1)
                    for t in range(TC):
                        act.wait_ge(down_made, ch * TC + t + 1)
                        c.stand_alone(act)
                        act.activation(c.y[:, bass.ds(ch * TC + t, 1), :], c.psum[:, 4 + t:5 + t, 0:D], ACT.Copy,
                                       scale=UNSCALE).then_inc(y_ready, 1)

            @block.vector
            def _(dve):
                with dve.Fori(0, CH) as ch:
                    for ht in range(HT + 1):
                        if ht < HT:
                            n = ch * HT + ht
                            dve.wait_ge(sig_ready, n + 1)
                            g = sig[:, ht % 2, :]
                            if not quantised:
                                dve.scalar_tensor_tensor(out=gate[:, ht % 2, :], in0=hidden(0, ht), scalar=UNSCALE * UNSCALE,
                                                         in1=g, op0=ALU.mult, op1=ALU.mult).then_inc(gate_ready, 1)
                                dve.wait_ge(gate_ready, n + 1)
                                g = gate[:, ht % 2, :]
                            dve.wait_ge(up_made, n + 1)
                            if ht >= 2:
                                dve.wait_ge(hid_lo, n - 1)
                            dve.tensor_tensor(hid[:, ht % 2, :], hidden(1, ht), g, ALU.mult).then_inc(hid_ready, 1)
                        if ht >= 1:
                            n = ch * HT + ht - 1
                            dve.wait_ge(hid_hi, n + 1)
                            dve.tensor_tensor(hidT[1][:, ht - 1, :], hid[:, (ht - 1) % 2, :], hidT[0][:, ht - 1, :],
                                              ALU.subtract).then_inc(hid_lo, 1)


def ffn_0(c, ins):
    ffn(c, "f0", F0, [ins[f"L0_ffn_w{j}"] for j in (1, 2, 3)], True)


def ffn_1(c, ins):
    ffn(c, "f1", F1, [ins[f"L1_ffn_w_{n}"] for n in ("gate", "up", "down")], False)


def attention_1(c, ins):
    nc = c.nc
    SCALE = float(HD1) ** -0.5
    J = H1 // G1
    R = P // J
    CH = B * S // BANK
    CB = S // BANK
    ONE = HD1
    with ExitStack() as ctx:
        sb = lambda n, shape, dt=F32: c.sb(f"a1_{n}", shape, dt, ctx)
        sem = lambda n: c.sem(f"a1_{n}")
        q_part = [sb(f"q_part{i}", [P, KT, B * S], F16) for i in range(2)]
        k_part = [sb(f"k_part{i}", [P, B * S], F16) for i in range(2)]
        v_all = sb("v_all", [P, NT, G1 * HD1])
        sel_q = [sb(f"sel_q{i}", [P, KT, G1, P], F16) for i in range(2)]
        sel_k = [sb(f"sel_k{i}", [P, G1, P], F16) for i in range(2)]
        ident_h = sb("ident_h", [P, P], F16)
        minus_row = sb("minus_row", [P, 1])
        wo_part = [sb(f"wo_part{i}", [P, KT, D], F16) for i in range(2)]
        kd = sb("kd", [P, 2, J, S], F16)
        qp, qf = sb("qp", [P, 2, S], F16), sb("qf", [P, 2, S], F16)
        kp = sb("kp", [P, 2, BANK], F16)
        vg = sb("vg", [P, 2, TB, R])
        mcol = sb("mcol", [P, TB, P], F16)
        mx = sb("mx", [P, TB, J, 2])
        att = c.y

        with ExitStack() as pctx:
            psb = lambda n, shape, dt=F32: c.sb(f"a1_{n}", shape, dt, pctx)
            cos, sin = psb("cos", [P, S]), psb("sin", [P, S])
            NW = {"q": D, "k": G1 * HD1, "v": G1 * HD1, "o": D}
            raw = {n: psb(f"raw_{n}", [P, KT, w]) for n, w in NW.items()}
            part = {n: [psb(f"w{n}{i}", [P, KT, NW[n]], F16) for i in range(2)] for n in "qkv"}
            part["o"] = wo_part
            swapped = {n: [psb(f"w{n}s{i}", [P, KT, NW[n]], F16) for i in range(2)] for n in "qk"}
            tcos, tsin, rope = (psb(n, [P, 2, BANK]) for n in ("tcos", "tsin", "rope"))
            loaded, consts, zeroed = sem("loaded"), sem("consts"), sem("zeroed")
            whi, wlo, wswap = sem("whi"), sem("wlo"), sem("wswap")
            made, cos_done, sin_done, rope_done, hi_done, lo_done, v_made, v_done = (
                sem(n) for n in ("made", "cos_done", "sin_done", "rope_done", "hi_done", "lo_done", "v_made", "v_done"))
            jobs = [(n, m) for n, m in (("q", 0), ("q", 1), ("k", 0))]
            NJ = len(jobs)

            with nc.Block() as block:
                @block.sync
                def _(sp):
                    for n in "qkvo":
                        sp.dma_start(raw[n][:, :, :], ins[f"L1_attn_w{n}"].rearrange("(k p) o -> p k o", p=P)).then_inc(loaded, 16)
                    sp.dma_start(cos[:, :], ins["rope1_cos"]).then_inc(consts, 16)
                    sp.dma_start(sin[:, :], ins["rope1_sin"]).then_inc(consts, 16)
                    for i in range(2):
                        sp.dma_start(sel_q[i][:, :, :, :], ins["sel_q"][i]).then_inc(consts, 16)
                        sp.dma_start(sel_k[i][:, :, :], ins["sel_k"][i]).then_inc(consts, 16)
                    sp.dma_start(minus_row[:, :], ins["minus_row"]).then_inc(consts, 16)
                    sp.wait_ge(consts, 112)

                @block.gpsimd
                def _(pool):
                    pool.memset(kd[:, 0, :, :].bitcast(F32), 0.0).then_inc(zeroed, 1)
                    pool.memset(kd[:, 1, :, :].bitcast(F32), 0.0).then_inc(zeroed, 1)
                    for i in range(2):
                        pool.memset(vg[:, i, :, :], 0.0).then_inc(zeroed, 1)
                    pool.memset(mcol[:, :, :], 0.0).then_inc(zeroed, 1)
                    for i in range(2):
                        pool.wait_ge(zeroed, 5 + i)
                        pool.memset(k_part[i][64:128, :], 0.0).then_inc(zeroed, 1)
                    pool.wait_ge(zeroed, 7)
                    pool.memset(vg[:, :, :, ONE:ONE + 1], 1.0).then_inc(zeroed, 1)
                    pool.wait_ge(zeroed, 8)

                @block.scalar
                def _(act):
                    act.activation(ident_h[:, :], c.ident[:, :], ACT.Copy)
                    act.wait_ge(loaded, 64)
                    for n in "qkvo":
                        act.activation(part[n][0][:, :, :], raw[n][:, :, :], ACT.Copy, scale=WSCALE).then_inc(whi, 1)
                    act.wait_ge(wlo, 2)
                    for n in "qk":
                        for i in range(2):
                            for e in range(2):
                                v = lambda w: w[:, :, :].rearrange("p k (o e) -> p k o e", e=2)
                                act.activation(v(swapped[n][i])[:, :, :, e], v(part[n][i])[:, :, :, 1 - e],
                                               ACT.Copy).then_inc(wswap, 1)
                    for half in range(2):
                        act.wait_ge(v_made, half + 1)
                        act.activation(v_all[:, half * 8:half * 8 + 8, :],
                                       c.psum[:, 6 + half, :].rearrange("p (t o) -> p t o", t=8), ACT.Copy,
                                       scale=1.0 / WSCALE).then_inc(v_done, 1)
                    act.wait_ge(v_done, 2)
                    with act.Fori(0, CH) as ch:
                        for m, (n, tile) in enumerate(jobs):
                            rows = 64 if n == "k" else P
                            tok = bass.ds(ch * BANK, BANK)
                            act.wait_ge(rope_done, ch * NJ + m + 1)
                            c.stand_alone(act)
                            dst = k_part[0][0:rows, tok] if n == "k" else q_part[0][:, tile, tok]
                            act.activation(dst, rope[0:rows, m % 2, :], ACT.Copy).then_inc(hi_done, 1)
                            act.wait_ge(lo_done, ch * NJ + m + 1)

                @block.tensor
                def _(pe):
                    pe.wait_ge(wlo, 3)
                    for t in range(NT):
                        terms = [(k, a, w) for k in range(KT) for a, w in ((0, 0), (0, 1), (1, 0))]
                        for n, (k, a, w) in enumerate(terms):
                            last = pe.matmul(c.psum[:, 6 + t // 8, (t % 8) * 64:(t % 8) * 64 + 64],
                                             (c.xT_hi, c.xT_lo)[a][:, k, t * P:(t + 1) * P], part["v"][w][:, k, :],
                                             start=(n == 0), stop=(n == len(terms) - 1))
                        if t % 8 == 7:
                            last.then_inc(v_made, 1)
                    pe.wait_ge(wswap, 8)
                    with pe.Fori(0, CH) as ch:
                        tok = bass.ds(ch * BANK, BANK)
                        for m, (n, tile) in enumerate(jobs):
                            rows = 64 if n == "k" else P
                            for s, ww in enumerate((part, swapped)):
                                terms = [(k, w, a) for k in range(KT) for w, a in ((0, 0), (0, 1), (1, 0))]
                                for i, (k, w, a) in enumerate(terms):
                                    last = pe.matmul(c.psum[0:rows, 2 * m + s, :],
                                                     ww[n][w][:, k, tile * P:tile * P + rows],
                                                     (c.xT_hi, c.xT_lo)[a][:, k, tok],
                                                     start=(i == 0), stop=(i == len(terms) - 1))
                            last.then_inc(made, 1)
                        pe.wait_ge(sin_done, ch * NJ + NJ)

                @block.vector
                def _(dve):
                    dve.wait_ge(loaded, 64)
                    for i, n in enumerate("qkvo"):
                        dve.wait_ge(whi, i + 1)
                        dve.scalar_tensor_tensor(out=part[n][1][:, :, :], in0=raw[n][:, :, :], scalar=WSCALE,
                                                 in1=part[n][0][:, :, :], op0=ALU.mult, op1=ALU.subtract).then_inc(wlo, 1)
                    dve.wait_ge(consts, 112)
                    with dve.Fori(0, B) as b:
                        for cb in range(CB):
                            for m, (n, tile) in enumerate(jobs):
                                rows = 64 if n == "k" else P
                                done = b * (CB * NJ) + cb * NJ + m
                                pos = slice(cb * BANK, (cb + 1) * BANK)
                                tok = bass.ds(b * S + cb * BANK, BANK)
                                dve.wait_ge(made, done + 1)
                                dve.tensor_tensor(tcos[0:rows, m % 2, :], c.psum[0:rows, 2 * m, :], cos[0:rows, pos], ALU.mult).then_inc(cos_done, 1)
                                dve.tensor_tensor(tsin[0:rows, m % 2, :], c.psum[0:rows, 2 * m + 1, :], sin[0:rows, pos], ALU.mult).then_inc(sin_done, 1)
                                dve.wait_ge(cos_done, done + 1)
                                dve.wait_ge(sin_done, done + 1)
                                dve.tensor_tensor(rope[0:rows, m % 2, :], tcos[0:rows, m % 2, :], tsin[0:rows, m % 2, :], ALU.add).then_inc(rope_done, 1)
                                dve.wait_ge(hi_done, done + 1)
                                hi_ = k_part[0][0:rows, tok] if n == "k" else q_part[0][:, tile, tok]
                                lo_ = k_part[1][0:rows, tok] if n == "k" else q_part[1][:, tile, tok]
                                dve.tensor_tensor(lo_, rope[0:rows, m % 2, :], hi_, ALU.subtract).then_inc(lo_done, 1)
                                dve.wait_ge(lo_done, done + 1)

        NP = 2 * J
        SUB = TB * J
        KEYS = [("kx", 0), ("kx", 1)]
        QS = [("qx", 0), ("qx", 1)]
        SCAN = []
        for t in range(TB):
            for p0 in range((t * P) // BANK + 1):
                n = min(BANK, (t + 1) * P - p0 * BANK)
                per = BANK // n if n <= BANK // 2 else 1
                per = J if n == P else per
                SCAN += [("scan", t, p0, j, per) for j in range(0, J, per)]
        MTS = [("mt", 0), ("mt", 1)]
        TURNS = [("ot", 0), ("ot", 1)]
        PREP = KEYS + QS + SCAN + MTS
        ALL = KEYS + QS + TURNS + SCAN + MTS

        def spread(items):
            total = sum(TB - kt for kt in range(TB))
            out, at, cols = [], 0, 0
            for s in range(SUB):
                cols += (TB - s // J) / J
                upto = min(len(items), -(-len(items) * cols // total)) if s < SUB - 1 else len(items)
                upto = int(upto)
                out.append(items[at:upto])
                at = upto
            return out

        FIRST_UNIT, ANY_UNIT, LAST_UNIT = spread(PREP), spread(ALL), spread(TURNS)
        N_FIRST, N_HEAD = 2 * len(PREP) + len(ALL), 2 * len(ALL)
        assert N_FIRST % 2 == 0 and len(ALL) % 2 == 0

        with ExitStack() as actx:
            asb = lambda n, shape, dt=F32: c.sb(f"a1_{n}", shape, dt, actx)
            prob = asb("prob", [P, NP, S])
            o_sb = asb("o_sb", [P, 2, S])
            rsum = asb("rsum", [P, TB // 2, J])
            work_ready, work_free = [sem(f"work_ready{i}") for i in range(2)], [sem(f"work_free{i}") for i in range(2)]
            kp_ready, kd_ready, qp_ready, vg_ready, mx_ready, mcol_ready, qf_ready = (
                sem(n) for n in ("kp_ready", "kd_ready", "qp_ready", "vg_ready", "mx_ready", "mcol_ready", "qf_ready"))
            scores_ready, prob_ready, context_done, o_ready = (
                sem(n) for n in ("scores_ready", "prob_ready", "context_done", "o_ready"))
            rsum_ready, att_ready, turned = sem("rsum_ready"), sem("att_ready"), sem("turned")

            def work(slot, a, b_):
                return c.psum[:, 6 + slot, a:b_]

            def turn(number):
                return number[1] % 2, number[0] + number[1] // 2

            def run(eng, do_item, step=lambda *a: None, unit_end=None, before_item=None):
                def unit(g, b, number, steps):
                    for s in range(SUB):
                        step(2 * g + b, b, s // J, s % J)
                        for n, item in enumerate(steps[s]):
                            if before_item:
                                before_item(2 * g + b, b, s, n, len(steps[s]))
                            do_item(item, number, g, b)
                            number = (number[0], number[1] + 1)
                        if before_item:
                            before_item(2 * g + b, b, s, len(steps[s]), len(steps[s]))
                    if unit_end:
                        unit_end(2 * g + b, b)
                    return number

                number = (0, 0)
                for item in PREP:
                    do_item(item, number, -1, 1)
                    number = (0, number[1] + 1)
                number = unit(0, 0, number, FIRST_UNIT)
                number = unit(0, 1, number, ANY_UNIT)
                assert number[1] == N_FIRST
                with eng.Fori(1, G1 - 1) as g:
                    base = ((g - 1) * (N_HEAD // 2) + N_FIRST // 2, 0)
                    unit(g, 1, unit(g, 0, base, ANY_UNIT), ANY_UNIT)
                number = ((G1 - 2) * (N_HEAD // 2) + N_FIRST // 2, 0)
                number = unit(G1 - 1, 1, unit(G1 - 1, 0, number, ANY_UNIT), LAST_UNIT)
                for item in TURNS:
                    do_item(item, number, G1, 0)
                    number = (number[0], number[1] + 1)

            def at(index, n=1):
                return slice(index * n, index * n + n) if isinstance(index, int) else bass.ds(index * n, n)

            def n_mx(t):
                return sum(1 for i in SCAN if i[1] < t)

            with nc.Block() as block:
                @block.tensor
                def _(pe):
                    def do_item(item, number, g, b):
                        slot, before = turn(number)
                        wait(pe, work_free[slot], before)
                        wb, kind = 1 - b, item[0]
                        wg = g + 1 if b else g
                        w = 2 * g + b + 1
                        if kind == "kx":
                            tok = slice(wb * S + item[1] * BANK, wb * S + (item[1] + 1) * BANK)
                            for i in range(2):
                                last = pe.matmul(work(slot, 0, BANK), sel_k[i][:, at(wg), :], k_part[i][:, tok],
                                                 start=(i == 0), stop=(i == 1))
                        elif kind == "qx":
                            tok = slice(wb * S + item[1] * BANK, wb * S + (item[1] + 1) * BANK)
                            for n, (k, i) in enumerate([(k, i) for k in range(KT) for i in range(2)]):
                                last = pe.matmul(work(slot, 0, BANK), sel_q[i][:, k, at(wg), :], q_part[i][:, k, tok],
                                                 start=(n == 0), stop=(n == 2 * KT - 1))
                        elif kind == "scan":
                            _, t, p0, j0, per = item
                            pe.wait_ge(kd_ready, w * 2 * J + 2 * J)
                            pe.wait_ge(qp_ready, w * 2 + 2)
                            a, e = p0 * BANK, min((p0 + 1) * BANK, (t + 1) * P)
                            edge, n = e == (t + 1) * P, e - a
                            for i in range(per):
                                last = pe.matmul(work(slot, i * n, i * n + n), qp[:, wb, t * P:(t + 1) * P],
                                                 kd[:, wb, j0 + i, a:e], start=True, stop=not edge)
                                if edge:
                                    last = pe.matmul(work(slot, (i + 1) * n - P, (i + 1) * n), c.ident_b[:, :],
                                                     c.mask_qk[:, :], start=False, stop=True)
                        elif kind == "mt":
                            pe.wait_ge(mcol_ready, w * TB + 4 * item[1] + 4)
                            for i in range(4):
                                last = pe.matmul(work(slot, i * P, (i + 1) * P), mcol[:, 4 * item[1] + i, :], ident_h[:, :],
                                                 start=True, stop=True)
                        elif kind == "ot":
                            pe.wait_ge(o_ready, 2 * g + b)
                            for i in range(4):
                                last = pe.transpose(work(slot, i * P, (i + 1) * P),
                                                    o_sb[:, 1 - b, (4 * item[1] + i) * P:(4 * item[1] + i + 1) * P], c.ident[:, :])
                        last.then_inc(work_ready[slot], 1)

                    def scores(kt, j, a, e):
                        return c.psum[:, 2 * (j % 2) + a // BANK, a % BANK:a % BANK + e - a]

                    def make_scores(u, b, kt, j):
                        s = kt * J + j
                        if s == 0:
                            pe.wait_ge(qf_ready, u * 2 + 2)
                        wait(pe, prob_ready, u * SUB + s - 1)
                        for n, (a, e) in enumerate(spans(kt * P, S)):
                            last = pe.matmul(scores(kt, j, a, e), kd[:, b, j, kt * P:(kt + 1) * P], qf[:, b, a:e],
                                             start=True, stop=(n > 0))
                            if n == 0:
                                last = pe.matmul(scores(kt, j, a, a + P), c.ident_b[:, :], c.mask_kq[:, :], start=False, stop=True)
                        last.then_inc(scores_ready, 1)

                    def before_item(u, b, s, i, n):
                        if s == 0 and i == min(1, n):
                            make_scores(u, b, 0, 0)
                        if s + 1 < SUB and i == (min(2, n) if s == 0 else min(1, n)):
                            make_scores(u, b, (s + 1) // J, (s + 1) % J)
                        if i == n and s >= J and s % J == 1:
                            make_context(u, b, s // J - 1)
                        if i == n and s == SUB - 1:
                            make_context(u, b, TB - 1)

                    def make_context(u, b, kt):
                        pe.wait_ge(prob_ready, u * SUB + kt * J + J)
                        pe.wait_ge(vg_ready, u + 1)
                        if kt == 0:
                            wait(pe, o_ready, u)
                        for a, e in spans(kt * P, S):
                            for i in range(J):
                                out = c.psum[i * R:(i + 1) * R, 4 + a // BANK, a % BANK:a % BANK + e - a]
                                last = pe.matmul(out, vg[:, b, kt, :], prob[:, J * (kt % 2) + i, a:e],
                                                 start=(kt == 0), stop=(kt == (e - 1) // P))
                        last.then_inc(context_done, 1)

                    run(pe, do_item, before_item=before_item)

                @block.scalar
                def _(act):
                    def do_item(item, number, g, b):
                        slot, before = turn(number)
                        wb, w = 1 - b, 2 * g + b + 1
                        if item[0] == "qx":
                            act.wait_ge(work_ready[slot], before + 1)
                            act.activation(qp[:, wb, item[1] * BANK:(item[1] + 1) * BANK], work(slot, 0, BANK),
                                           ACT.Copy).then_inc(qp_ready, 1)
                            act.wait_ge(qp_ready, w * 2 + item[1] + 1)
                            act.sem_inc(work_free[slot], 1)
                            if item[1] == 1:
                                wait(act, context_done, (w - 1) * TB)
                                wg = g + 1 if b else g
                                c.stand_alone(act)
                                act.activation(vg[:, wb, :, 0:HD1], v_all[:, wb * TB:(wb + 1) * TB, at(wg, HD1)],
                                               ACT.Copy).then_inc(vg_ready, 1)

                    def step(u, b, kt, j):
                        s = kt * J + j
                        act.wait_ge(scores_ready, u * SUB + s + 1)
                        wait(act, context_done, u * TB + kt - 1)
                        pair = c.psum[:, 2 * (j % 2):2 * (j % 2) + 2, :].rearrange("p b n -> p (b n)")
                        act.activation(prob[:, s % NP, kt * P:S], pair[:, kt * P:S], ACT.Exp, scale=SCALE).then_inc(prob_ready, 1)

                    def unit_end(u, b):
                        act.wait_ge(context_done, u * TB + TB)
                        wait(act, turned, (u - 1) * 2)
                        act.activation(o_sb[:, b, :], c.psum[:, 4:6, :].rearrange("p b n -> p (b n)"),
                                       ACT.Copy).then_inc(o_ready, 1)

                    run(act, do_item, step, unit_end)

                @block.vector
                def _(dve):
                    def do_item(item, number, g, b):
                        slot, before = turn(number)
                        wb, w, kind = 1 - b, 2 * g + b + 1, item[0]
                        if kind == "qx":
                            return
                        dve.wait_ge(work_ready[slot], before + 1)
                        if kind == "kx":
                            i = item[1]
                            cols = slice(i * BANK, (i + 1) * BANK)
                            dve.tensor_copy(kp[:, i, :], work(slot, 0, BANK)).then_inc(kp_ready, 1)
                            dve.wait_ge(kp_ready, w * 2 + i + 1)
                            dve.sem_inc(work_free[slot], 1)
                            if i == 0:
                                wait(dve, scores_ready, (w - 1) * SUB)
                            for j in range(J):
                                rows = slice(j * R, (j + 1) * R)
                                dve.tensor_scalar(kd[rows, wb, j, cols], kp[rows, i, :], minus_row[rows, 0:1], None,
                                                  ALU.add).then_inc(kd_ready, 1)
                        elif kind == "scan":
                            _, t, p0, j0, per = item
                            a, e = p0 * BANK, min((p0 + 1) * BANK, (t + 1) * P)
                            n = e - a
                            index = SCAN.index(item)
                            if index == 0:
                                wait(dve, mcol_ready, w * TB)
                            dve.tensor_reduce(mx[:, t, j0:j0 + per, p0], work(slot, 0, per * n).rearrange("p (j n) -> p j n", j=per),
                                              AX.X, ALU.max).then_inc(mx_ready, 1)
                            dve.wait_ge(mx_ready, w * len(SCAN) + index + 1)
                            dve.sem_inc(work_free[slot], 1)
                            if index + 1 == n_mx(t + 1):
                                dst = mcol[:, t, :].rearrange("p (j r) -> p j r", j=J)[:, :, 3 * HD1]
                                if t == 0:
                                    wait(dve, qf_ready, w * 2)
                                if t * P < BANK:
                                    dve.tensor_copy(dst, mx[:, t, :, 0]).then_inc(mcol_ready, 1)
                                else:
                                    dve.tensor_tensor(dst, mx[:, t, :, 0], mx[:, t, :, 1], ALU.max).then_inc(mcol_ready, 1)
                        elif kind == "mt":
                            i = item[1]
                            cols = slice(i * BANK, (i + 1) * BANK)
                            dve.tensor_tensor(qf[:, wb, cols], work(slot, 0, BANK), qp[:, wb, cols], ALU.add).then_inc(qf_ready, 1)
                            dve.wait_ge(qf_ready, w * 2 + i + 1)
                            dve.sem_inc(work_free[slot], 1)
                        elif kind == "ot":
                            i = item[1]
                            pu, pb = 2 * g + b - 1, 1 - b
                            v = work(slot, 0, BANK).rearrange("p (t j r) -> p t j r", t=4, j=J)
                            wait(dve, att_ready, pu * 2 + i)
                            dve.reciprocal(rsum[:, :, :], v[:, :, :, ONE]).then_inc(rsum_ready, 1)
                            dve.wait_ge(rsum_ready, pu * 2 + i + 1)
                            pg = g - 1 if b == 0 else g
                            dst = att[:, pb * TB + 4 * i:pb * TB + 4 * i + 4, at(pg, J * HD1)].rearrange("p t (j d) -> p t j d", j=J)
                            dve.tensor_tensor(dst, v[:, :, :, 0:HD1], rsum[:, :, :].unsqueeze(3).broadcast_to([P, 4, J, HD1]),
                                              ALU.mult).then_inc(att_ready, 1)
                            dve.wait_ge(att_ready, pu * 2 + i + 1)
                            dve.sem_inc(work_free[slot], 1)
                            dve.sem_inc(turned, 1)

                    run(dve, do_item)

        at_turned, at_hi, at_lo, y_made, y_out = (sem(n) for n in ("at_turned", "at_hi", "at_lo", "y_made", "y_out"))
        GRP, PER = 2, 4
        with nc.Block() as block:
            @block.tensor
            def _(pe):
                for m in range(NT // GRP):
                    wait(pe, at_lo, m - 1)
                    for j in range(GRP):
                        for k in range(KT):
                            last = pe.transpose(c.psum[:, m % 2, k * GRP * P + j * P:k * GRP * P + (j + 1) * P],
                                                att[:, m * GRP + j, k * P:(k + 1) * P], c.ident[:, :])
                    last.then_inc(at_turned, 1)
                pe.wait_ge(at_lo, NT // GRP)
                with pe.Fori(0, NT // PER) as i:
                    for j in range(PER):
                        for n, (k, w, a) in enumerate([(k, w, a) for k in range(KT) for w, a in ((0, 0), (0, 1), (1, 0))]):
                            last = pe.matmul(c.psum[:, 4 + j, 0:D], (c.xT_hi, c.xT_lo)[a][:, k, bass.ds((i * PER + j) * P, P)],
                                             wo_part[w][:, k, :], start=(n == 0), stop=(n == 3 * KT - 1))
                        last.then_inc(y_made, 1)
                    pe.wait_ge(y_out, i * PER + PER)

            @block.scalar
            def _(act):
                with act.Fori(0, NT // PER) as i:
                    for g in range(PER // GRP):
                        m = i * 2 + g
                        act.wait_ge(at_turned, m + 1)
                        c.stand_alone(act)
                        act.activation(c.xT_hi[:, :, bass.ds(m * GRP * P, GRP * P)],
                                       c.psum[:, g, :].rearrange("p (k n) -> p k n", k=KT), ACT.Copy).then_inc(at_hi, 1)
                with act.Fori(0, NT // PER) as i:
                    for j in range(PER):
                        t = i * PER + j
                        act.wait_ge(y_made, t + 1)
                        c.stand_alone(act)
                        act.activation(c.y[:, bass.ds(t, 1), :], c.psum[:, 4 + j:5 + j, 0:D], ACT.Copy, scale=1.0 / WSCALE).then_inc(y_out, 1)

            @block.vector
            def _(dve):
                with dve.Fori(0, NT // PER) as i:
                    for g in range(PER // GRP):
                        m = i * 2 + g
                        span = bass.ds(m * GRP * P, GRP * P)
                        dve.wait_ge(at_hi, m + 1)
                        dve.tensor_tensor(c.xT_lo[:, :, span], c.psum[:, g, :].rearrange("p (k n) -> p k n", k=KT),
                                          c.xT_hi[:, :, span], ALU.subtract).then_inc(at_lo, 1)


_INS = ["L0_attn_hidden_states", "L0_attn_Wq", "L0_attn_bq", "L0_attn_Wk", "L0_attn_bk", "L0_attn_Wv", "L0_attn_bv",
        "L0_attn_Wo", "L0_attn_bo", "L0_ffn_w1", "L0_ffn_w2", "L0_ffn_w3", "L1_attn_wq", "L1_attn_wk", "L1_attn_wv",
        "L1_attn_wo", "L1_ffn_w_gate", "L1_ffn_w_up", "L1_ffn_w_down"]


def shape_constants():
    import numpy as np

    def angles(width):
        exponent = np.arange(0, width, 2, dtype=np.float32) / np.float32(width)
        inv_freq = (np.float32(1.0) / np.power(np.float32(10000.0), exponent)).astype(np.float32)
        return np.arange(S, dtype=np.float32)[:, None] * inv_freq[None, :]

    a0 = angles(HD0).T
    tables = {
        "rope0_cos": np.concatenate([np.cos(a0)] * 2, 0),
        "rope0_sin": np.concatenate([np.sin(a0), -np.sin(a0)], 0),
    }
    a1 = np.repeat(angles(HD1).T, 2, 0)
    sign = np.where(np.arange(HD1) % 2 == 0, -1.0, 1.0).astype(np.float32)[:, None]
    tables["rope1_cos"] = np.tile(np.cos(a1), (P // HD1, 1)) / np.float32(WSCALE)
    tables["rope1_sin"] = np.tile(np.sin(a1) * sign, (P // HD1, 1)) / np.float32(WSCALE)
    tables = {k: np.ascontiguousarray(v, dtype=np.float32) for k, v in tables.items()}
    rep, rows = H1 // G1, P // (H1 // G1)
    sel_q = np.zeros((2, P, KT, G1, P), np.float16)
    sel_k = np.zeros((2, P, G1, P), np.float16)
    for g in range(G1):
        for j in range(rep):
            for d in range(HD1):
                q_row = (g * rep + j) * HD1 + d
                for copy, (q_part, k_part) in enumerate(((0, 0), (0, 1), (1, 0))):
                    sel_q[q_part, q_row % P, q_row // P, g, j * rows + copy * HD1 + d] = 1.0
                    sel_k[k_part, g * HD1 + d, g, j * rows + copy * HD1 + d] = 1.0
    tables["sel_q"], tables["sel_k"] = sel_q, sel_k
    minus = np.zeros((P, 1), np.float32)
    minus[3 * HD1::rows] = -1.0
    tables["minus_row"] = minus
    return tables


def kernel(**inputs):
    import numpy as _np
    import concourse.bacc as _bacc
    from concourse import mybir as _mybir
    from concourse.bass_utils import run_bass_kernel_spmd as _run

    nc = _bacc.Bacc("TRN2", target_bir_lowering=False, num_devices=1)
    arrays, args = {}, {}
    inputs = dict(inputs)
    for n in ("L0_attn_bq", "L0_attn_bk"):
        inputs[n] = _np.asarray(inputs[n]).reshape(H0, HD0).T
    for n in ("L0_attn_Wq", "L0_attn_Wk", "L0_attn_Wv", "L0_attn_Wo"):
        inputs[n] = _np.asarray(inputs[n]).T
    for name, a in list(inputs.items()) + list(shape_constants().items()):
        a = _np.ascontiguousarray(a)
        arrays[f"in_{name}_dram"] = a
        args[name] = nc.dram_tensor(f"in_{name}_dram", a.shape, _mybir.dt.from_np(a.dtype), kind="ExternalInput").ap()
    out = nc.dram_tensor("out_0_dram", (B, S, D), F32, kind="ExternalOutput").ap()
    program(nc, args, out)
    r = _run(nc, [arrays], core_ids=[0])
    return r.results[0]["out_0_dram"]
```

```python
from contextlib import ExitStack

import concourse.bass as bass
from concourse import mybir

F32 = mybir.dt.float32
F16 = mybir.dt.float16
BF16 = mybir.dt.bfloat16
ALU = mybir.AluOpType
ACT = mybir.ActivationFunctionType
AX = mybir.AxisListType

P = 128
B, S, D = 2, 1024, 256
NT = B * S // P
TB = S // P
KT = D // P
BANK = 512
EPS = 1e-5
WSCALE = 64.0
MASKED = -1e30

H0, HD0 = 16, 128
F0 = 704
H1, G1, HD1 = 32, 8, 8
F1 = 1024


class Core:

    def __init__(self, nc, ctx):
        self.nc = nc
        self.ctx = ctx
        self.x = self.sb("x", [P, NT, D], F32)
        self.y = self.sb("y", [P, NT, D], F32)
        self.xT_hi = self.sb("xT_hi", [P, KT, B * S], F16)
        self.xT_lo = self.sb("xT_lo", [P, KT, B * S], F16)
        self.ident = self.sb("ident", [P, P], F32)
        self.ident_b = self.sb("ident_b", [P, P], BF16)
        self.ones_b = self.sb("ones_b", [P, P], BF16)
        self.ones = self.sb("ones", [P, P], F32)
        self.scale_b = self.sb("scale_b", [P, 1], BF16)
        self.mask_kq = self.sb("mask_kq", [P, P], BF16)
        self.mask_qk = self.sb("mask_qk", [P, P], BF16)
        self.sems = []
        self.passed = nc.alloc_semaphore(name="passed")
        self.psum = ctx.enter_context(nc.psum_tensor("psum", [P, 8, BANK], F32))

    def sb(self, name, shape, dt, ctx=None):
        return (ctx or self.ctx).enter_context(self.nc.sbuf_tensor(name, shape, dt))

    def sem(self, name):
        self.sems.append(self.nc.alloc_semaphore(name=name))
        return self.sems[-1]

    def stand_alone(self, eng):
        eng.sem_inc(self.passed, 1)

    def end_phase(self):
        self.nc.all_engine_barrier()
        self.nc.clear_and_free_semaphores(self.sems)
        self.nc.all_engine_barrier()
        self.sems = []


def constants(c, x_in):
    nc = c.nc
    x_loaded, filled, selected = c.sem("x_loaded"), c.sem("filled"), c.sem("selected")
    with nc.Block() as block:
        @block.sync
        def _(sp):
            xv = x_in.rearrange("b (t p) d -> p (b t) d", p=P)
            for q in range(4):
                sp.dma_start(c.x[:, 4 * q:4 * q + 4, :], xv[:, 4 * q:4 * q + 4, :]).then_inc(x_loaded, 16)
            sp.wait_ge(x_loaded, 64)

        @block.gpsimd
        def _(pool):
            for buf, value in ((c.ident, 0.0), (c.ident_b, 0.0), (c.mask_kq, 0.0), (c.mask_qk, 0.0),
                               (c.ones_b, 1.0), (c.ones, 1.0), (c.scale_b, WSCALE)):
                pool.memset(buf[:, :], value).then_inc(filled, 1)
            pool.wait_ge(filled, 7)
            for buf in (c.ident, c.ident_b):
                pool.affine_select(out=buf[:, :], in_=buf[:, :], compare_op=ALU.not_equal, fill=1.0,
                                   base=0, pattern=[[-1, P]], channel_multiplier=1).then_inc(selected, 1)
            pool.affine_select(out=c.mask_kq[:, :], in_=c.mask_kq[:, :], compare_op=ALU.is_ge, fill=MASKED,
                               base=0, pattern=[[1, P]], channel_multiplier=-1).then_inc(selected, 1)
            pool.affine_select(out=c.mask_qk[:, :], in_=c.mask_qk[:, :], compare_op=ALU.is_ge, fill=MASKED,
                               base=0, pattern=[[-1, P]], channel_multiplier=1).then_inc(selected, 1)
            pool.wait_ge(selected, 4)


TPC = BANK // P
CHUNKS = NT // TPC


def wait(eng, sem, value):
    if not (isinstance(value, int) and value <= 0):
        eng.wait_ge(sem, value)


def run_steps(eng, depth, step):
    for s in range(depth - 1):
        step(s)
    with eng.Fori(depth - 1, CHUNKS) as s:
        step(s)
    for s in range(CHUNKS, CHUNKS + depth - 1):
        step(s)


def has_chunk(s, stage):
    return not isinstance(s, int) or 0 <= s - stage < CHUNKS


class Norm:
    STEPS = 9

    def __init__(self, c, name, ctx):
        sb = lambda n, *shape: c.sb(f"{name}_{n}", [P, TPC, *shape], F32, ctx)
        self.stats = sb("stats", 6)
        (self.msum, self.mdif, self.sq, self.m2, self.var, self.sd, self.inv, self.quo, self.avg, self.half,
         self.rstd, self.shift) = (sb(n) for n in ("msum", "mdif", "sq", "m2", "var", "sd", "inv", "quo", "avg",
                                                   "half", "rstd", "shift"))
        self.stats_ready, self.step, self.var_ready, self.sd_ready, self.norm_ready = (
            c.sem(f"{name}_{n}") for n in ("stats_ready", "step", "var_ready", "sd_ready", "norm_ready"))
        self.c = c

    def then_wait(self, dve, ch, k, ins):
        ins.then_inc(self.step, 1)
        dve.wait_ge(self.step, ch * self.STEPS + k)

    def variance(self, dve, src, ch):
        wait(dve, self.norm_ready, 2 * ch)
        self.c.stand_alone(dve)
        for j in range(TPC):
            dve.bn_stats(self.stats[:, j, :], src[:, bass.ds(ch * TPC + j, 1), :]).then_inc(self.stats_ready, 1)
        dve.wait_ge(self.stats_ready, ch * TPC + TPC)
        mean, square = (lambda h: self.stats[:, :, 1 + 3 * h]), (lambda h: self.stats[:, :, 2 + 3 * h])
        dve.tensor_tensor(self.msum[:, :], mean(0), mean(1), ALU.add).then_inc(self.step, 1)
        dve.tensor_tensor(self.m2[:, :], square(0), square(1), ALU.add).then_inc(self.step, 1)
        self.then_wait(dve, ch, 3, dve.tensor_tensor(self.mdif[:, :], mean(0), mean(1), ALU.subtract))
        dve.tensor_scalar(self.m2[:, :], self.m2[:, :], 1.0 / D, EPS, ALU.mult, ALU.add).then_inc(self.step, 1)
        self.then_wait(dve, ch, 5, dve.tensor_tensor(self.sq[:, :], self.mdif[:, :], self.mdif[:, :], ALU.mult))
        dve.scalar_tensor_tensor(out=self.var[:, :], in0=self.sq[:, :], scalar=0.25, in1=self.m2[:, :],
                                 op0=ALU.mult, op1=ALU.add).then_inc(self.var_ready, 1)

    def root(self, act, ch):
        act.wait_ge(self.var_ready, ch + 1)
        act.activation(self.sd[:, :], self.var[:, :], ACT.Sqrt).then_inc(self.sd_ready, 1)

    def normaliser(self, dve, ch, applied):
        dve.wait_ge(self.var_ready, ch + 1)
        dve.wait_ge(self.sd_ready, ch + 1)
        wait(dve, applied, ch * TPC)
        self.then_wait(dve, ch, 6, dve.reciprocal(self.inv[:, :], self.sd[:, :]))
        self.then_wait(dve, ch, 7, dve.tensor_tensor(self.quo[:, :], self.var[:, :], self.inv[:, :], ALU.mult))
        self.then_wait(dve, ch, 8, dve.tensor_tensor(self.avg[:, :], self.quo[:, :], self.sd[:, :], ALU.add))
        self.then_wait(dve, ch, 9, dve.reciprocal(self.half[:, :], self.avg[:, :]))
        dve.scalar_tensor_tensor(out=self.shift[:, :], in0=self.msum[:, :], scalar=-1.0, in1=self.half[:, :],
                                 op0=ALU.mult, op1=ALU.mult).then_inc(self.norm_ready, 1)
        dve.tensor_scalar(self.rstd[:, :], self.half[:, :], 2.0, None, ALU.mult).then_inc(self.norm_ready, 1)

    def apply(self, act, ch, j, dst, src, done):
        act.activation(dst, src, ACT.Identity, bias=self.shift[:, j:j + 1], scale=self.rstd[:, j:j + 1]).then_inc(done, 1)


class AddNorm:

    def __init__(self, c, name, ctx):
        self.c, self.norm = c, Norm(c, f"{name}_y", ctx)
        self.y_normed, self.x_added = c.sem(f"{name}_y_normed"), c.sem(f"{name}_x_added")

    def variance(self, dve, ch):
        self.norm.variance(dve, self.c.y, ch)

    def normaliser(self, dve, ch):
        self.norm.normaliser(dve, ch, self.y_normed)

    def apply(self, act, ch):
        act.wait_ge(self.norm.norm_ready, 2 * ch + 2)
        self.c.stand_alone(act)
        for j in range(TPC):
            tile = self.c.y[:, bass.ds(ch * TPC + j, 1), :]
            self.norm.apply(act, ch, j, tile, tile, self.y_normed)

    def add(self, pool, ch):
        for j in range(TPC):
            t = ch * TPC + j
            pool.wait_ge(self.y_normed, t + 1)
            pool.tensor_tensor(self.c.x[:, bass.ds(t, 1), :], self.c.x[:, bass.ds(t, 1), :],
                               self.c.y[:, bass.ds(t, 1), :], ALU.add).then_inc(self.x_added, 1)


class Extra:
    sync = tensor = scalar_first = gpsimd_first = lambda self, eng: None
    gpsimd = scalar = vector = lambda self, eng, s: None

    def has_matrix(self, s, stage):
        return not isinstance(s, int) or 0 <= s - stage < 3


class Loads(Extra):

    def __init__(self, loads):
        self.sync = loads


def boundary(c, name, add_y, extra=None):
    GRP = 2
    NG = TPC // GRP
    X = 1 if add_y else 0
    with ExitStack() as ctx:
        xn = c.sb(f"{name}_xn", [P, TPC, D], F32, ctx)
        add = AddNorm(c, name, ctx) if add_y else None
        norm = Norm(c, f"{name}_x", ctx)
        xn_ready, turned, hi_ready, lo_ready = (
            c.sem(f"{name}_{n}") for n in ("xn_ready", "turned", "hi_ready", "lo_ready"))

        with c.nc.Block() as block:
            @block.vector
            def _(dve):
                def step(s):
                    if add_y and has_chunk(s, 0):
                        add.variance(dve, s)
                    if has_chunk(s, X):
                        if add_y:
                            dve.wait_ge(add.x_added, (s - X) * TPC + TPC)
                        norm.variance(dve, c.x, s - X)
                    if add_y and has_chunk(s, 0):
                        add.normaliser(dve, s)
                    if has_chunk(s, X):
                        norm.normaliser(dve, s - X, xn_ready)
                    if has_chunk(s, X + 1):
                        for g in range(NG):
                            m = (s - X - 1) * NG + g
                            span = bass.ds(m * GRP * P, GRP * P)
                            dve.wait_ge(hi_ready, m + 1)
                            dve.tensor_tensor(c.xT_lo[:, :, span], c.psum[:, g, :].rearrange("p (k n) -> p k n", k=KT),
                                              c.xT_hi[:, :, span], ALU.subtract).then_inc(lo_ready, 1)
                    if extra:
                        extra.vector(dve, s)
                run_steps(dve, X + 2, step)
                dve.wait_ge(lo_ready, NT // GRP)

            @block.scalar
            def _(act):
                if extra:
                    extra.scalar_first(act)

                def step(s):
                    if add_y and has_chunk(s, 0):
                        add.norm.root(act, s)
                    if has_chunk(s, X):
                        norm.root(act, s - X)
                    if add_y and has_chunk(s, 0):
                        add.apply(act, s)
                    if has_chunk(s, X):
                        ch = s - X
                        act.wait_ge(norm.norm_ready, 2 * ch + 2)
                        wait(act, turned, ch * NG)
                        c.stand_alone(act)
                        for j in range(TPC):
                            norm.apply(act, ch, j, xn[:, j:j + 1, :], c.x[:, bass.ds(ch * TPC + j, 1), :], xn_ready)
                        for g in range(NG):
                            m = ch * NG + g
                            act.wait_ge(turned, m + 1)
                            c.stand_alone(act)
                            act.activation(c.xT_hi[:, :, bass.ds(m * GRP * P, GRP * P)],
                                           c.psum[:, g, :].rearrange("p (k n) -> p k n", k=KT),
                                           ACT.Copy).then_inc(hi_ready, 1)
                    if extra:
                        extra.scalar(act, s)
                run_steps(act, X + 2, step)

            @block.tensor
            def _(pe):
                if extra:
                    extra.tensor(pe)

                def step(ch):
                    for g in range(NG):
                        m = ch * NG + g
                        pe.wait_ge(xn_ready, ch * TPC + g * GRP + GRP)
                        wait(pe, lo_ready, (ch - 1) * NG + g + 1)
                        for j in range(GRP):
                            for k in range(KT):
                                last = pe.transpose(c.psum[:, g, k * GRP * P + j * P:k * GRP * P + (j + 1) * P],
                                                    xn[:, g * GRP + j, k * P:(k + 1) * P], c.ident[:, :])
                        last.then_inc(turned, 1)
                step(0)
                with pe.Fori(1, CHUNKS) as ch:
                    step(ch)

            if add_y or extra:
                @block.gpsimd
                def _(pool):
                    def step(s):
                        if add_y and has_chunk(s, 0):
                            add.add(pool, s)
                        if extra:
                            extra.gpsimd(pool, s)
                    if extra:
                        extra.gpsimd_first(pool)
                    run_steps(pool, X + 2, step)

            if extra:
                @block.sync
                def _(sp):
                    extra.sync(sp)


def program(nc, ins, out):
    with ExitStack() as ctx:
        c = Core(nc, ctx)
        constants(c, ins["L0_attn_hidden_states"])
        with ExitStack() as wctx:
            raw = RawWeights(c, "f0", F0, [ins[f"L0_ffn_w{j}"] for j in (1, 2, 3)], wctx)
            attention_0(c, ins, lambda loads: boundary(c, "in", False, LoadPadded(c, raw, loads)))
            c.end_phase()
            weights = Quantise(c, raw, wctx)
            boundary(c, "mid1", True, weights)
            ffn(c, "f0", raw.tiles, weights.parts, 1.0, True)
        c.end_phase()
        attention_1(c, ins, lambda loads: boundary(c, "mid2", False, Loads(loads)))
        c.end_phase()
        with ExitStack() as wctx:
            raw = RawWeights(c, "f1", F1, [ins[f"L1_ffn_w_{n}"] for n in ("gate", "up", "down")], wctx)
            weights = LoadAndSplit(c, raw, wctx)
            boundary(c, "mid3", True, weights)
            ffn(c, "f1", raw.tiles, weights.parts, 1.0 / WSCALE, False, out)


def spans(lo, hi):
    while lo < hi:
        end = min(hi, (lo // BANK + 1) * BANK)
        yield lo, end
        lo = end


def attention_0(c, ins, before):
    nc = c.nc
    SCALE = float(HD0) ** -0.5
    CH = S // BANK
    NP = 4
    inner = H0 * HD0
    w_in = [ins[f"L0_attn_W{n}"].rearrange("(k p) o -> p k o", p=P) for n in "qkv"]
    wo_in = ins["L0_attn_Wo"]

    PREP = [("proj", 0, 0), ("proj", 0, 1), ("proj", 1, 0), ("proj", 1, 1)]
    VALS = [("vals", 0), ("vals", 1)]
    SUMS = [("sums",)]
    OUTS = [("out", i) for i in range(TB // 2)]
    SCAN = [("scan", (0, 0), (1, 0))] + [("scan", (t, n)) for t in range(2, TB) for n in range((t * P) // BANK + 1)]
    ITEMS = [PREP, VALS[0:1], VALS[1:2] + SCAN[0:2], SCAN[2:3] + SUMS + SCAN[3:4], OUTS[0:1] + SCAN[4:6], OUTS[1:2] + SCAN[6:8],
             OUTS[2:3] + SCAN[8:10], SCAN[10:11] + OUTS[3:4]]
    FIRST = PREP + VALS + SCAN
    no_out = [[i for i in s if i[0] not in ("sums", "out")] for s in ITEMS]
    only_out = [[i for i in s if i[0] in ("sums", "out")] for s in ITEMS]
    count = lambda steps: sum(map(len, steps))
    N_FIRST = len(FIRST) + count(no_out) + count(ITEMS)
    N_HEAD = 2 * count(ITEMS)
    assert N_FIRST % 2 == 0 and count(ITEMS) % 2 == 0

    with ExitStack() as ctx:
        sb = lambda n, shape, dt=F32: c.sb(f"a0_{n}", shape, dt, ctx)
        sem = lambda n: c.sem(f"a0_{n}")
        cos, sin = sb("cos", [P, S]), sb("sin", [P, S])
        w_raw = sb("w_raw", [P, 3, KT, P])
        w_hi, w_lo = sb("w_hi", [P, 3, KT, P], F16), sb("w_lo", [P, 3, KT, P], F16)
        wo_raw = sb("wo_raw", [P, D])
        wo_hi, wo_lo = sb("wo_hi", [P, D], F16), sb("wo_lo", [P, D], F16)
        bias, head_bias = sb("bias", [P, 2, H0]), sb("head_bias", [P, 2])
        bias_v = sb("bias_v", [P, inner])
        lin, rot, cosd, rope = (sb(n, [P, 2, BANK]) for n in ("lin", "rot", "cosd", "rope"))
        hi = {0: sb("q_hi", [P, 2, S], F16), 1: sb("k_hi", [P, 2, S], F16)}
        lo = {0: sb("q_lo", [P, 2, S], F16), 1: sb("k_lo", [P, 2, S], F16)}
        val = sb("val", [P, 2, TB, HD0])
        mx, mx_all = sb("mx", [P, 2, TB, 2]), sb("mx_all", [P, 2, TB])
        diag = sb("diag", [P, 2, S], BF16)
        prob = sb("prob", [P, NP, S])
        psumk = sb("psumk", [P, 2, S])
        psumk_hi, psumk_lo = sb("psumk_hi", [P, S], F16), sb("psumk_lo", [P, S], F16)
        ctx_hi, ctx_lo = sb("ctx_hi", [P, 2, S], F16), sb("ctx_lo", [P, 2, S], F16)
        rsum = sb("rsum", [P, 2, TB])

        tables, w_loaded, wo_loaded, bias_loaded = sem("tables"), sem("w_loaded"), sem("wo_loaded"), sem("bias_loaded")
        w_used, bias_ready = sem("w_used"), sem("bias_ready")
        biasv_loaded, y_started = sem("biasv_loaded"), sem("y_started")
        work_ready, work_free = [sem(f"work_ready{i}") for i in range(2)], [sem(f"work_free{i}") for i in range(2)]
        whi_ready, wlo_ready = sem("whi_ready"), sem("wlo_ready")
        sums_hi, sums_lo = sem("sums_hi"), sem("sums_lo")
        cosd_ready, rot_ready, rope_ready, lin_ready = sem("cosd_ready"), sem("rot_ready"), sem("rope_ready"), sem("lin_ready")
        rhi_ready, qk_ready, v_ready = sem("rhi_ready"), sem("qk_ready"), sem("v_ready")
        joined, diag_ready = sem("joined"), sem("diag_ready")
        scores_ready, prob_ready, context_done, summed = sem("scores_ready"), sem("prob_ready"), sem("context_done"), sem("summed")
        chi_ready, ctx_ready, rsum_ready, out_done = sem("chi_ready"), sem("ctx_ready"), sem("rsum_ready"), sem("out_done")
        wohi_ready, wo_ready = sem("wohi_ready"), sem("wo_ready")

        def work(slot, a, b):
            return c.psum[:, 6 + slot, a:b]

        def scores(kt, a, b):
            bank = 2 * (kt % 2) + a // BANK
            return c.psum[:, bank, a % BANK:a % BANK + b - a]

        def scores_row(kt, a):
            pair = c.psum[:, 2 * (kt % 2):2 * (kt % 2) + 2, :].rearrange("p b n -> p (b n)")
            return pair[:, a:S]

        def context(a, b):
            return c.psum[:, 4 + a // BANK, a % BANK:a % BANK + b - a]

        def run(eng, do_item, step_begin, step_end, weights=None, unit_end=None, before_item=None):
            def unit(h, b, number, steps, next_unit):
                for kt in range(TB):
                    step_begin(2 * h + b, b, kt)
                    for n, item in enumerate(steps[kt]):
                        if before_item:
                            before_item(2 * h + b, b, kt, n, len(steps[kt]))
                        do_item(item, number, h, b, next_unit)
                        number = (number[0], number[1] + 1)
                    if before_item:
                        before_item(2 * h + b, b, kt, len(steps[kt]), len(steps[kt]))
                    step_end(2 * h + b, b, kt)
                    if weights and b == 0 and kt == 3 and not (isinstance(h, int) and h == H0 - 1):
                        weights(h)
                if unit_end:
                    unit_end(h, b)
                return number

            number = (0, 0)
            if weights:
                weights(-1)
            for item in FIRST:
                do_item(item, number, -1, 1, 0)
                number = (0, number[1] + 1)
            number = unit(0, 0, number, no_out, 1)
            number = unit(0, 1, number, ITEMS, 2)
            assert number[1] == N_FIRST
            with eng.Fori(1, H0 - 1) as h:
                number = ((h - 1) * (N_HEAD // 2) + N_FIRST // 2, 0)
                number = unit(h, 0, number, ITEMS, 2 * h + 1)
                unit(h, 1, number, ITEMS, 2 * h + 2)
            number = ((H0 - 2) * (N_HEAD // 2) + N_FIRST // 2, 0)
            number = unit(H0 - 1, 0, number, ITEMS, 2 * H0 - 1)
            number = unit(H0 - 1, 1, number, only_out, None)
            for item in SUMS + OUTS:
                do_item(item, number, H0, 0, None)
                number = (number[0], number[1] + 1)

        def column(index, n=1):
            return slice(index * n, index * n + n) if isinstance(index, int) else bass.ds(index * n, n)

        def turn(number):
            return number[1] % 2, number[0] + number[1] // 2

        def load_head(sp, h, at):
            wait(sp, w_used, h)
            for j in range(3):
                sp.dma_start(w_raw[:, j, :, :], w_in[j][:, :, at]).then_inc(w_loaded, 16)

        def first_loads(sp):
            load_head(sp, 0, slice(0, P))
            for j, n in enumerate("qk"):
                sp.dma_start(bias[:, j, :], ins[f"L0_attn_b{n}"]).then_inc(bias_loaded, 16)
            sp.dma_start(cos[:, :], ins["rope0_cos"]).then_inc(tables, 16)
            sp.dma_start(sin[:, :], ins["rope0_sin"]).then_inc(tables, 16)
            sp.dma_start(bias_v[:, :], ins["L0_attn_bv"].rearrange("(a i) -> a i", a=1).broadcast_to([P, inner])).then_inc(biasv_loaded, 16)
            sp.dma_start(wo_raw[:, :], wo_in[0:P, :]).then_inc(wo_loaded, 16)
            sp.dma_start(c.y[:, :, :], ins["L0_attn_bo"].rearrange("(a t i) -> a t i", a=1, t=1).broadcast_to([P, NT, D])).then_inc(y_started, 16)

        before(first_loads)

        with nc.Block() as block:
            @block.sync
            def _(sp):
                with sp.Fori(1, H0) as h:
                    load_head(sp, h, bass.ds(sp.snap(h * P), P))

            @block.tensor
            def _(pe):
                def do_item(item, number, h, b, w):
                    slot, before = turn(number)
                    wait(pe, work_free[slot], before)
                    kind = item[0]
                    if kind == "proj":
                        _, j, ch = item
                        wb = 1 - b
                        pe.wait_ge(wlo_ready, (h + 1 if b else h) * 3 + 1 + j)
                        tok = slice(wb * S + ch * BANK, wb * S + (ch + 1) * BANK)
                        terms = [(w_hi, c.xT_hi), (w_hi, c.xT_lo), (w_lo, c.xT_hi)]
                        for n, (a, m, k) in enumerate([(a, m, k) for k in range(KT) for a, m in terms]):
                            last = pe.matmul(work(slot, 0, BANK), a[:, j, k, :], m[:, k, tok],
                                             start=(n == 0), stop=(n == 3 * KT - 1))
                    elif kind == "vals":
                        wb = 1 - b
                        pe.wait_ge(wlo_ready, (h + 1 if b else h) * 3 + 3)
                        for t in range(4):
                            tok = slice(wb * S + (item[1] * 4 + t) * P, wb * S + (item[1] * 4 + t + 1) * P)
                            n = 0
                            for k in range(KT):
                                for m, a in ((c.xT_hi, w_hi), (c.xT_hi, w_lo), (c.xT_lo, w_hi)):
                                    last = pe.matmul(work(slot, t * P, (t + 1) * P), m[:, k, tok], a[:, 2, k, :],
                                                     start=(n == 0), stop=(n == 3 * KT - 1))
                                    n += 1
                    elif kind == "scan":
                        wb = 1 - b
                        pe.wait_ge(qk_ready, w * 4 + 4)
                        col = 0
                        for t, part in item[1:]:
                            a, e = part * BANK, min((part + 1) * BANK, (t + 1) * P)
                            edge = e == (t + 1) * P
                            last = pe.matmul(work(slot, col, col + e - a), hi[0][:, wb, t * P:(t + 1) * P],
                                             hi[1][:, wb, a:e], start=True, stop=not edge)
                            col += e - a
                            if edge:
                                last = pe.matmul(work(slot, col - P, col), c.ident_b[:, :], c.mask_qk[:, :],
                                                 start=False, stop=True)
                    elif kind == "sums":
                        pu, pb = 2 * h + b - 1, 1 - b
                        pe.wait_ge(sums_lo, pu + 1)
                        for t in range(TB):
                            for n, part in enumerate((psumk_hi, psumk_lo)):
                                last = pe.matmul(work(slot, t, t + 1), part[:, t * P:(t + 1) * P], c.scale_b[:, 0:1],
                                                 start=(n == 0), stop=(n == 1))
                    elif kind == "out":
                        pu, pb = 2 * h + b - 1, 1 - b
                        pe.wait_ge(ctx_ready, pu + 1)
                        pe.wait_ge(wo_ready, h if b == 0 else h + 1)
                        for t in range(2):
                            tt = item[1] * 2 + t
                            for n, (a, m) in enumerate(((ctx_hi, wo_hi), (ctx_hi, wo_lo), (ctx_lo, wo_hi))):
                                last = pe.matmul(work(slot, t * D, (t + 1) * D), a[:, pb, tt * P:(tt + 1) * P], m[:, :],
                                                 start=(n == 0), stop=(n == 2))
                    last.then_inc(work_ready[slot], 1)

                def make_scores(u, b, kt):
                    if kt == 0:
                        pe.wait_ge(diag_ready, u * TB + TB)
                    wait(pe, prob_ready, u * TB + kt - 1)
                    keys = slice(kt * P, (kt + 1) * P)
                    pieces = list(spans(kt * P, S))
                    for n, (a, e) in enumerate(pieces):
                        terms = [(hi[1][:, b, keys], hi[0]), (hi[1][:, b, keys], lo[0]), (lo[1][:, b, keys], hi[0])]
                        for m, (kk, qq) in enumerate(terms):
                            pe.matmul(scores(kt, a, e), kk, qq[:, b, a:e], start=(m == 0), stop=False)
                        if n == 0:
                            pe.matmul(scores(kt, a, a + P), c.ident_b[:, :], c.mask_kq[:, :], start=False, stop=False)
                        last = pe.matmul(scores(kt, a, e), c.ones_b[:, :], diag[:, b, a:e], start=False, stop=True)
                    last.then_inc(scores_ready, 1)

                def before_item(u, b, kt, i, n):
                    first = min(1, n)
                    if kt == 0 and i == first:
                        make_scores(u, b, 0)
                    if kt + 1 < TB and i == (min(2, n) if kt == 0 else first):
                        make_scores(u, b, kt + 1)
                    if i == (n if kt == 0 or n < 3 else n - 1):
                        make_context(u, b, kt)

                def make_context(u, b, kt):
                    pe.wait_ge(prob_ready, u * TB + kt + 1)
                    if kt == 0:
                        wait(pe, ctx_ready, u)
                    for a, e in spans(kt * P, S):
                        last = pe.matmul(context(a, e), val[:, b, kt, :], prob[:, kt % NP, a:e],
                                         start=(kt == 0), stop=(kt == (min(e, S) - 1) // P))
                    last.then_inc(context_done, 1)

                run(pe, do_item, lambda *a: None, lambda *a: None, before_item=before_item)

            @block.scalar
            def _(act):
                def do_item(item, number, h, b, w):
                    slot, before = turn(number)
                    kind = item[0]
                    if kind == "proj":
                        _, j, ch = item
                        n = w * 4 + 2 * j + ch
                        act.wait_ge(work_ready[slot], before + 1)
                        wait(act, qk_ready, n - 1)
                        if j == 0 and ch == 0:
                            act.wait_ge(bias_ready, (h + 1 if b else h) + 1)
                        act.activation(lin[:, ch, :], work(slot, 0, BANK), ACT.Identity, bias=head_bias[:, j:j + 1],
                                       scale=1.0 / WSCALE).then_inc(lin_ready, 1)

                def weights(h):
                    act.wait_ge(w_loaded, (h + 1) * 48 + 48)
                    wait(act, v_ready, (h + 1) * 4)
                    for j in range(3):
                        act.activation(w_hi[:, j, :, :], w_raw[:, j, :, :], ACT.Copy, scale=WSCALE).then_inc(whi_ready, 1)

                def step_begin(u, b, kt):
                    act.wait_ge(scores_ready, u * TB + kt + 1)
                    wait(act, context_done, u * TB + kt - NP + 1)
                    wait(act, summed, u * TB + kt - NP + (2 if kt == NP else 1))
                    act.activation(prob[:, kt % NP, kt * P:S], scores_row(kt, kt * P), ACT.Exp,
                                   scale=SCALE).then_inc(prob_ready, 1)

                def split_sums(pu, pb):
                    act.wait_ge(summed, pu * TB + TB)
                    wait(act, rsum_ready, pu)
                    act.activation(psumk_hi[:, :], psumk[:, pb, :], ACT.Copy).then_inc(sums_hi, 1)

                def step_end(u, b, kt):
                    if kt == 0 and not (isinstance(u, int) and u == 0):
                        split_sums(u - 1, 1 - b)

                def unit_end(h, b):
                    u = 2 * h + b
                    act.wait_ge(context_done, u * TB + TB)
                    wait(act, out_done, u - 1)
                    act.activation(ctx_hi[:, b, :], c.psum[:, 4:6, :].rearrange("p b n -> p (b n)"),
                                   ACT.Copy).then_inc(chi_ready, 1)
                    if b == 0:
                        if not (isinstance(h, int) and h == 0):
                            act.wait_ge(out_done, u)
                        act.wait_ge(wo_loaded, 16 * (h + 1))
                        act.activation(wo_hi[:, :], wo_raw[:, :], ACT.Copy, scale=WSCALE).then_inc(wohi_ready, 1)
                    elif not (isinstance(h, int) and h == H0 - 1):
                        act.wait_ge(wo_ready, h + 1)
                        act.dma_start(wo_raw[:, :], wo_in[column(h + 1, P), :]).then_inc(wo_loaded, 16)

                run(act, do_item, step_begin, step_end, weights, unit_end)
                split_sums(2 * H0 - 1, 1)

            @block.vector
            def _(dve):
                dve.wait_ge(tables, 32)
                dve.wait_ge(y_started, 16)
                dve.wait_ge(biasv_loaded, 16)
                dve.wait_ge(bias_loaded, 32)

                def do_item(item, number, h, b, w):
                    slot, before = turn(number)
                    kind = item[0]
                    wb = 1 - b
                    if kind == "proj":
                        _, j, ch = item
                        n = w * 4 + 2 * j + ch
                        tok = slice(ch * BANK, (ch + 1) * BANK)
                        dve.wait_ge(lin_ready, n + 1)
                        dve.sem_inc(work_free[slot], 1)
                        wait(dve, qk_ready, n - 1)
                        dve.tensor_tensor(rot[0:64, ch, :], lin[64:128, ch, :], sin[64:128, tok], ALU.mult).then_inc(rot_ready, 1)
                        dve.tensor_tensor(rot[64:128, ch, :], lin[0:64, ch, :], sin[0:64, tok], ALU.mult).then_inc(rot_ready, 1)
                        dve.wait_ge(rot_ready, n * 2 + 2)
                        dve.wait_ge(cosd_ready, n + 1)
                        dve.tensor_tensor(rope[:, ch, :], rot[:, ch, :], cosd[:, ch, :], ALU.add).then_inc(rope_ready, 1)
                        dve.wait_ge(rope_ready, n + 1)
                        if j == 0 and ch == 0:
                            wait(dve, scores_ready, w * TB - TB)
                        dve.tensor_copy(hi[j][:, wb, tok], rope[:, ch, :]).then_inc(rhi_ready, 1)
                        dve.wait_ge(rhi_ready, n + 1)
                        dve.tensor_tensor(lo[j][:, wb, tok], rope[:, ch, :], hi[j][:, wb, tok], ALU.subtract).then_inc(qk_ready, 1)
                    elif kind == "vals":
                        i = item[1]
                        dve.wait_ge(work_ready[slot], before + 1)
                        if i == 0:
                            wait(dve, context_done, w * TB - TB)
                        dve.scalar_tensor_tensor(out=val[:, wb, 4 * i:4 * i + 4, :],
                                                 in0=work(slot, 0, BANK).rearrange("p (t n) -> p t n", t=4),
                                                 scalar=1.0 / WSCALE,
                                                 in1=bias_v[:, column(h + 1 if b else h, HD0)].unsqueeze(1).broadcast_to([P, 4, HD0]),
                                                 op0=ALU.mult, op1=ALU.add).then_inc(v_ready, 1)
                        dve.wait_ge(v_ready, w * 2 + i + 1)
                        dve.sem_inc(work_free[slot], 1)
                    elif kind == "scan":
                        dve.wait_ge(work_ready[slot], before + 1)
                        col = 0
                        for t, part in item[1:]:
                            n = min(BANK, (t + 1) * P - part * BANK)
                            last = dve.tensor_reduce(mx[:, wb, t, part:part + 1], work(slot, col, col + n), AX.X, ALU.max)
                            col += n
                        last.then_inc(work_free[slot], 1)
                        dve.wait_ge(work_free[slot], before + 1)
                        for t, part in item[1:]:
                            two = t * P >= BANK
                            if two and part == 0:
                                continue
                            top = mx[:, wb, t, 0:1]
                            if two:
                                top = mx_all[:, wb, t:t + 1]
                                dve.tensor_tensor(top, mx[:, wb, t, 0:1], mx[:, wb, t, 1:2], ALU.max).then_inc(joined, 1)
                                dve.wait_ge(joined, w * (TB // 2) + t - TB // 2 + 1)
                            if t == 0:
                                wait(dve, scores_ready, w * TB - TB)
                            dve.tensor_scalar(diag[:, wb, t * P:(t + 1) * P], c.ident_b[:, :], top, -1.0,
                                              ALU.mult, ALU.mult).then_inc(diag_ready, 1)
                    elif kind == "sums":
                        pu, pb = 2 * h + b - 1, 1 - b
                        dve.wait_ge(work_ready[slot], before + 1)
                        dve.reciprocal(rsum[:, pb, :], work(slot, 0, TB)).then_inc(rsum_ready, 1)
                        dve.wait_ge(rsum_ready, pu + 1)
                        dve.sem_inc(work_free[slot], 1)
                    elif kind == "out":
                        pu, pb = 2 * h + b - 1, 1 - b
                        dve.wait_ge(work_ready[slot], before + 1)
                        if item[1] == 0:
                            wait(dve, out_done, pu)
                        for t in range(2):
                            tt = item[1] * 2 + t
                            yt = c.y[:, pb * TB + tt, :]
                            last = dve.scalar_tensor_tensor(out=yt, in0=work(slot, t * D, (t + 1) * D), scalar=rsum[:, pb, tt:tt + 1],
                                                            in1=yt, op0=ALU.mult, op1=ALU.add)
                        last.then_inc(work_free[slot], 1)
                        if item[1] == TB // 2 - 1:
                            dve.wait_ge(work_free[slot], before + 1)
                            dve.sem_inc(out_done, 1)

                def weights(h):
                    for j in range(3):
                        dve.wait_ge(whi_ready, (h + 1) * 3 + j + 1)
                        dve.scalar_tensor_tensor(out=w_lo[:, j, :, :], in0=w_raw[:, j, :, :], scalar=WSCALE, in1=w_hi[:, j, :, :],
                                                 op0=ALU.mult, op1=ALU.subtract).then_inc(wlo_ready, 1)
                    dve.tensor_scalar(head_bias[:, :], bias[:, :, column(h + 1)], 1.0, None, ALU.mult).then_inc(bias_ready, 1)
                    dve.wait_ge(wlo_ready, (h + 1) * 3 + 3)
                    dve.sem_inc(w_used, 1)

                def unit_end(h, b):
                    dve.wait_ge(chi_ready, 2 * h + b + 1)
                    dve.tensor_tensor(ctx_lo[:, b, :], c.psum[:, 4:6, :].rearrange("p b n -> p (b n)"), ctx_hi[:, b, :],
                                      ALU.subtract).then_inc(ctx_ready, 1)
                    if b == 0:
                        dve.wait_ge(wohi_ready, h + 1)
                        dve.scalar_tensor_tensor(out=wo_lo[:, :], in0=wo_raw[:, :], scalar=WSCALE, in1=wo_hi[:, :],
                                                 op0=ALU.mult, op1=ALU.subtract).then_inc(wo_ready, 1)

                run(dve, do_item, lambda *a: None, lambda *a: None, weights, unit_end)

            @block.gpsimd
            def _(pool):
                pool.wait_ge(tables, 32)

                def do_item(item, number, h, b, w):
                    if item[0] == "proj":
                        _, j, ch = item
                        n = w * 4 + 2 * j + ch
                        slot, before = turn(number)
                        pool.wait_ge(lin_ready, n + 1)
                        wait(pool, rope_ready, n - 1)
                        pool.tensor_tensor(cosd[:, ch, :], lin[:, ch, :], cos[:, ch * BANK:(ch + 1) * BANK],
                                           ALU.mult).then_inc(cosd_ready, 1)

                def split_sums(pu, pb):
                    pool.wait_ge(sums_hi, pu + 1)
                    pool.tensor_tensor(psumk_lo[:, :], psumk[:, pb, :], psumk_hi[:, :], ALU.subtract).then_inc(sums_lo, 1)

                def step_end(u, b, kt):
                    if kt == 0 and not (isinstance(u, int) and u == 0):
                        split_sums(u - 1, 1 - b)
                    pool.wait_ge(prob_ready, u * TB + kt + 1)
                    if kt == 0:
                        wait(pool, out_done, u - 1)
                        pool.tensor_tensor(psumk[:, b, 0:P], prob[:, 0, 0:P], c.ones[:, :], ALU.mult).then_inc(summed, 1)
                    elif kt == 1:
                        pool.tensor_tensor(psumk[:, b, P:S], prob[:, 0, P:S], prob[:, 1, P:S], ALU.add).then_inc(summed, 1)
                    else:
                        pool.wait_ge(summed, u * TB + kt)
                        pool.tensor_tensor(psumk[:, b, kt * P:S], psumk[:, b, kt * P:S], prob[:, kt % NP, kt * P:S],
                                           ALU.add).then_inc(summed, 1)

                run(pool, do_item, lambda *a: None, step_end)
                split_sums(2 * H0 - 1, 1)


class RawWeights:

    def __init__(self, c, name, width, ins_w, ctx):
        self.name, self.width, self.ins_w = name, width, ins_w
        self.tiles = -(-width // P)
        self.cols = self.tiles * D
        self.buf = c.sb(f"{name}_raw", [P, 3, self.cols], F32, ctx)

    def view(self, buf, j):
        return buf[:, j, :].rearrange("p (k n) -> p k n", k=KT if j < 2 else self.tiles)

    def load(self, sp, loaded):
        full, rest = self.width // P, self.width % P
        count = 0
        for j in range(3):
            dst, src = self.view(self.buf, j), self.ins_w[j]
            if j < 2:
                pieces = [(dst[:, :, 0:self.width], src.rearrange("(k p) n -> p k n", p=P))]
            else:
                pieces = [(dst[:, 0:full, :], src[0:full * P, :].rearrange("(k p) n -> p k n", p=P))]
                if rest:
                    pieces.append((dst[0:rest, full, :], src[full * P:self.width, :]))
            for to, data in pieces:
                sp.dma_start(to, data).then_inc(loaded, 16)
                count += 16
        return count


class LoadPadded(Extra):

    def __init__(self, c, raw, loads):
        self.c, self.raw, self.loads = c, raw, loads
        self.padded, self.loaded = c.sem(f"{raw.name}_padded"), c.sem(f"{raw.name}_loaded")

    def sync(self, sp):
        self.loads(sp)
        sp.wait_ge(self.padded, 3)
        count = self.raw.load(sp, self.loaded)
        sp.wait_ge(self.loaded, count)

    def gpsimd_first(self, pool):
        raw = self.raw
        for j in range(3):
            buf = raw.view(raw.buf, j)
            pool.memset(buf[:, :, raw.width:raw.tiles * P] if j < 2 else buf[:, raw.width // P, :], 0.0).then_inc(self.padded, 1)


class Quantise(Extra):
    W_EPS = 1e-8

    def __init__(self, c, raw, ctx):
        self.c, self.raw = c, raw
        self.total = c.psum[:, 7, 0:3]
        self.scrap = c.sb("scrap", [P, raw.cols], F32, ctx)
        self.mag, self.gam, self.pos, self.neg = (c.sb(f"q_{n}", [P, 3], F32, ctx) for n in ("mag", "gam", "pos", "neg"))
        self.below = c.sb("below", [P, 3, raw.cols], F16, ctx)
        self.ternary = c.sb("ternary", [P, 3, raw.cols], F16, ctx)
        self.parts = [[raw.view(self.ternary, j)] for j in range(3)]
        self.mag_ready, self.total_ready, self.thr, self.below_ready, self.q_ready = (
            c.sem(n) for n in ("mag_ready", "total_ready", "thr", "below_ready", "q_ready"))

    def scalar_first(self, act):
        for j in range(3):
            wait(act, self.mag_ready, j)
            act.activation(self.scrap[:, :], self.raw.buf[:, j, :], ACT.Abs,
                           accum_out=self.mag[:, j:j + 1]).then_inc(self.mag_ready, 1)

    def tensor(self, pe):
        pe.wait_ge(self.mag_ready, 3)
        pe.matmul(self.total, self.c.ones[:, :], self.mag[:, :], start=True, stop=True).then_inc(self.total_ready, 1)

    def vector(self, dve, s):
        if isinstance(s, int) and s == 0:
            dve.wait_ge(self.total_ready, 1)
            dve.tensor_scalar(self.gam[:, :], self.total, 1.0 / (self.raw.width * D), self.W_EPS, ALU.mult, ALU.add).then_inc(self.thr, 1)
            dve.wait_ge(self.thr, 1)
            dve.tensor_scalar(self.pos[:, :], self.gam[:, :], 0.5, None, ALU.mult).then_inc(self.thr, 1)
            dve.tensor_scalar(self.neg[:, :], self.gam[:, :], -0.5, None, ALU.mult).then_inc(self.thr, 1)
            dve.wait_ge(self.thr, 3)
        if self.has_matrix(s, 2):
            j = bass.ds(s - 2, 1)
            dve.tensor_scalar(self.below[:, j, :], self.raw.buf[:, j, :], self.neg[:, j], None,
                              ALU.is_lt).then_inc(self.below_ready, 1)
            dve.wait_ge(self.below_ready, s - 1)
            dve.scalar_tensor_tensor(out=self.ternary[:, j, :], in0=self.raw.buf[:, j, :], scalar=self.pos[:, j],
                                     in1=self.below[:, j, :], op0=ALU.is_gt, op1=ALU.subtract).then_inc(self.q_ready, 1)


class LoadAndSplit(Extra):

    def __init__(self, c, raw, ctx):
        self.c, self.raw = c, raw
        self.part = [c.sb(f"w_{n}", [P, 3, raw.cols], F16, ctx) for n in ("hi", "lo")]
        self.parts = [[raw.view(part, j) for part in self.part] for j in range(3)]
        self.loaded, self.hi_made, self.lo_made = (c.sem(n) for n in ("w_loaded", "w_hi_made", "w_lo_made"))

    def sync(self, sp):
        assert self.raw.load(sp, self.loaded) == 48

    def scalar(self, act, s):
        if self.has_matrix(s, 1):
            if isinstance(s, int):
                act.wait_ge(self.loaded, 48)
            j = bass.ds(s - 1, 1)
            act.activation(self.part[0][:, j, :], self.raw.buf[:, j, :], ACT.Copy, scale=WSCALE).then_inc(self.hi_made, 1)

    def vector(self, dve, s):
        if self.has_matrix(s, 2):
            j = bass.ds(s - 2, 1)
            dve.wait_ge(self.hi_made, s - 1)
            dve.scalar_tensor_tensor(out=self.part[1][:, j, :], in0=self.raw.buf[:, j, :], scalar=WSCALE,
                                     in1=self.part[0][:, j, :], op0=ALU.mult, op1=ALU.subtract).then_inc(self.lo_made, 1)


def ffn(c, name, tiles, w_parts, unscale, sigmoid_only, out=None):
    HT = tiles
    WP = len(w_parts[0])
    TERMS = [(wi, xi) for wi in range(WP) for xi in range(2) if wi + xi <= 1]

    with ExitStack() as ctx:
        sb = lambda n, shape, dt=F32: c.sb(f"{name}_{n}", shape, dt, ctx)
        sem = lambda n: c.sem(f"{name}_{n}")
        sig, gate = sb("sig", [P, 2, BANK]), sb("gate", [P, 2, BANK])
        hid = sb("hid", [P, 2, BANK])
        hidT = [sb(f"hidT{i}", [P, HT, BANK], F16) for i in range(2)]
        gate_made, up_made, sig_ready, gate_ready, hid_ready, hid_hi, hid_lo = (
            sem(n) for n in ("gate_made", "up_made", "sig_ready", "gate_ready", "hid_ready", "hid_hi", "hid_lo"))
        down_made, y_ready, stored = sem("down_made"), sem("y_ready"), sem("stored")
        add = AddNorm(c, f"{name}_end", ctx)

        def hidden(j, ht):
            return c.psum[:, 2 * j + ht % 2, :]

        def run_chunks(eng, body, last=None):
            body(0, False)
            body(1, True)
            with eng.Fori(2, CHUNKS) as ch:
                body(ch, True)
            if last:
                last()

        with c.nc.Block() as block:
            @block.tensor
            def _(pe):
                def body(ch, _):
                    for ht in range(HT):
                        for j in range(2):
                            if ht >= 2:
                                pe.wait_ge(hid_ready, ch * HT + ht - 1)
                            for n, (k, wi, xi) in enumerate([(k, wi, xi) for k in range(KT) for wi, xi in TERMS]):
                                last = pe.matmul(hidden(j, ht), w_parts[j][wi][:, k, ht * P:(ht + 1) * P],
                                                 (c.xT_hi, c.xT_lo)[xi][:, k, bass.ds(ch * BANK, BANK)],
                                                 start=(n == 0), stop=(n == KT * len(TERMS) - 1))
                            last.then_inc((gate_made, up_made)[j], 1)
                    wait(pe, y_ready, ch * TPC)
                    for t in range(TPC):
                        for ht in range(HT):
                            if t == 0:
                                pe.wait_ge(hid_lo, ch * HT + ht + 1)
                            for n, (wi, xi) in enumerate(TERMS):
                                last = pe.matmul(c.psum[:, 4 + t, 0:D], hidT[xi][:, ht, t * P:(t + 1) * P], w_parts[2][wi][:, ht, :],
                                                 start=(ht == 0 and n == 0), stop=(ht == HT - 1 and n == len(TERMS) - 1))
                        last.then_inc(down_made, 1)
                run_chunks(pe, body)

            @block.scalar
            def _(act):
                def body(ch, add_last):
                    for ht in range(HT + 1):
                        if ht < HT:
                            n = ch * HT + ht
                            act.wait_ge(gate_made, n + 1)
                            if ht >= 2:
                                act.wait_ge(hid_ready, n - 1)
                            act.activation(sig[:, ht % 2, :], hidden(0, ht), ACT.Sigmoid, scale=unscale).then_inc(sig_ready, 1)
                        if ht >= 1:
                            n = ch * HT + ht - 1
                            act.wait_ge(hid_ready, n + 1)
                            act.activation(hidT[0][:, ht - 1, :], hid[:, (ht - 1) % 2, :], ACT.Copy).then_inc(hid_hi, 1)
                        if add_last and ht == 1:
                            add.norm.root(act, ch - 1)
                        if add_last and ht == 2:
                            add.apply(act, ch - 1)
                    for t in range(TPC):
                        act.wait_ge(down_made, ch * TPC + t + 1)
                        c.stand_alone(act)
                        act.activation(c.y[:, bass.ds(ch * TPC + t, 1), :], c.psum[:, 4 + t:5 + t, 0:D], ACT.Copy,
                                       scale=unscale).then_inc(y_ready, 1)

                def last():
                    add.norm.root(act, CHUNKS - 1)
                    add.apply(act, CHUNKS - 1)
                run_chunks(act, body, last)

            @block.vector
            def _(dve):
                def body(ch, add_last):
                    for ht in range(HT + 1):
                        if ht < HT:
                            n = ch * HT + ht
                            dve.wait_ge(sig_ready, n + 1)
                            g = sig[:, ht % 2, :]
                            if not sigmoid_only:
                                dve.scalar_tensor_tensor(out=gate[:, ht % 2, :], in0=hidden(0, ht), scalar=unscale * unscale,
                                                         in1=g, op0=ALU.mult, op1=ALU.mult).then_inc(gate_ready, 1)
                                dve.wait_ge(gate_ready, n + 1)
                                g = gate[:, ht % 2, :]
                            dve.wait_ge(up_made, n + 1)
                            if ht >= 2:
                                dve.wait_ge(hid_lo, n - 1)
                            dve.tensor_tensor(hid[:, ht % 2, :], hidden(1, ht), g, ALU.mult).then_inc(hid_ready, 1)
                        if ht >= 1:
                            n = ch * HT + ht - 1
                            dve.wait_ge(hid_hi, n + 1)
                            dve.tensor_tensor(hidT[1][:, ht - 1, :], hid[:, (ht - 1) % 2, :], hidT[0][:, ht - 1, :],
                                              ALU.subtract).then_inc(hid_lo, 1)
                        if add_last and ht == 0:
                            dve.wait_ge(y_ready, ch * TPC)
                            add.variance(dve, ch - 1)
                        if add_last and ht == 1:
                            add.normaliser(dve, ch - 1)

                def last():
                    dve.wait_ge(y_ready, NT)
                    add.variance(dve, CHUNKS - 1)
                    add.normaliser(dve, CHUNKS - 1)
                run_chunks(dve, body, last)

            @block.gpsimd
            def _(pool):
                with pool.Fori(0, CHUNKS) as ch:
                    add.add(pool, ch)
                pool.wait_ge(add.x_added, NT)

            if out is not None:
                @block.sync
                def _(sp):
                    ov = out.rearrange("b (t p) d -> p (b t) d", p=P)
                    for ch in range(CHUNKS):
                        sp.wait_ge(add.x_added, TPC * (ch + 1))
                        tiles = slice(TPC * ch, TPC * (ch + 1))
                        sp.dma_start(ov[:, tiles, :], c.x[:, tiles, :]).then_inc(stored, 16)
                    sp.wait_ge(stored, 16 * CHUNKS)


def attention_1(c, ins, before):
    nc = c.nc
    SCALE = float(HD1) ** -0.5
    J = H1 // G1
    R = P // J
    CH = B * S // BANK
    CB = S // BANK
    ONE = HD1
    with ExitStack() as ctx:
        sb = lambda n, shape, dt=F32: c.sb(f"a1_{n}", shape, dt, ctx)
        sem = lambda n: c.sem(f"a1_{n}")
        q_part = [sb(f"q_part{i}", [P, KT, B * S], F16) for i in range(2)]
        k_part = [sb(f"k_part{i}", [P, B * S], F16) for i in range(2)]
        v_all = sb("v_all", [P, NT, G1 * HD1])
        sel_q = [sb(f"sel_q{i}", [P, KT, G1, P], F16) for i in range(2)]
        sel_k = [sb(f"sel_k{i}", [P, G1, P], F16) for i in range(2)]
        ident_h = sb("ident_h", [P, P], F16)
        minus_row = sb("minus_row", [P, 1])
        wo_part = [sb(f"wo_part{i}", [P, KT, D], F16) for i in range(2)]
        kd = sb("kd", [P, 2, J, S], F16)
        qp, qf = sb("qp", [P, 2, S], F16), sb("qf", [P, 2, S], F16)
        kp = sb("kp", [P, 2, BANK], F16)
        vg = sb("vg", [P, 2, TB, R])
        mcol = sb("mcol", [P, TB, P], F16)
        mx = sb("mx", [P, TB, J, 2])
        att = c.y

        with ExitStack() as pctx:
            psb = lambda n, shape, dt=F32: c.sb(f"a1_{n}", shape, dt, pctx)
            cos, sin = psb("cos", [P, S]), psb("sin", [P, S])
            NW = {"q": D, "k": G1 * HD1, "v": G1 * HD1, "o": D}
            raw = {n: psb(f"raw_{n}", [P, KT, w]) for n, w in NW.items()}
            part = {n: [psb(f"w{n}{i}", [P, KT, NW[n]], F16) for i in range(2)] for n in "qkv"}
            part["o"] = wo_part
            swapped = {n: [psb(f"w{n}s{i}", [P, KT, NW[n]], F16) for i in range(2)] for n in "qk"}
            tcos, tsin, rope = (psb(n, [P, 3, BANK]) for n in ("tcos", "tsin", "rope"))
            loaded, consts, zeroed = sem("loaded"), sem("consts"), sem("zeroed")
            whi, wlo, wswap = sem("whi"), sem("wlo"), sem("wswap")
            made, cos_done, sin_done, rope_done, hi_done, lo_done, v_made, v_done = (
                sem(n) for n in ("made", "cos_done", "sin_done", "rope_done", "hi_done", "lo_done", "v_made", "v_done"))
            jobs = [(n, m) for n, m in (("q", 0), ("q", 1), ("k", 0))]
            NJ = len(jobs)

            def first_loads(sp):
                for n in "qkvo":
                    sp.dma_start(raw[n][:, :, :], ins[f"L1_attn_w{n}"].rearrange("(k p) o -> p k o", p=P)).then_inc(loaded, 16)
                sp.dma_start(cos[:, :], ins["rope1_cos"]).then_inc(consts, 16)
                sp.dma_start(sin[:, :], ins["rope1_sin"]).then_inc(consts, 16)
                for i in range(2):
                    sp.dma_start(sel_q[i][:, :, :, :], ins["sel_q"][i]).then_inc(consts, 16)
                    sp.dma_start(sel_k[i][:, :, :], ins["sel_k"][i]).then_inc(consts, 16)
                sp.dma_start(minus_row[:, :], ins["minus_row"]).then_inc(consts, 16)

            before(first_loads)

            with nc.Block() as block:
                @block.gpsimd
                def _(pool):
                    pool.memset(kd[:, 0, :, :].bitcast(F32), 0.0).then_inc(zeroed, 1)
                    pool.memset(kd[:, 1, :, :].bitcast(F32), 0.0).then_inc(zeroed, 1)
                    for i in range(2):
                        pool.memset(vg[:, i, :, :], 0.0).then_inc(zeroed, 1)
                    pool.memset(mcol[:, :, :], 0.0).then_inc(zeroed, 1)
                    for i in range(2):
                        pool.wait_ge(zeroed, 5 + i)
                        pool.memset(k_part[i][64:128, :], 0.0).then_inc(zeroed, 1)
                    pool.wait_ge(zeroed, 7)
                    pool.memset(vg[:, :, :, ONE:ONE + 1], 1.0).then_inc(zeroed, 1)
                    pool.wait_ge(zeroed, 8)
                    with pool.Fori(0, CH) as ch:
                        for m, (n, tile) in enumerate(jobs):
                            rows = 64 if n == "k" else P
                            pool.wait_ge(sin_done, ch * NJ + m + 1)
                            pool.wait_ge(cos_done, ch * NJ + m + 1)
                            pool.tensor_tensor(rope[0:rows, m, :], tcos[0:rows, m, :], tsin[0:rows, m, :], ALU.add).then_inc(rope_done, 1)

                @block.scalar
                def _(act):
                    act.activation(ident_h[:, :], c.ident[:, :], ACT.Copy)
                    act.wait_ge(loaded, 64)
                    for n in "qkvo":
                        act.activation(part[n][0][:, :, :], raw[n][:, :, :], ACT.Copy, scale=WSCALE).then_inc(whi, 1)
                    act.wait_ge(wlo, 2)
                    for n in "qk":
                        for i in range(2):
                            for e in range(2):
                                v = lambda w: w[:, :, :].rearrange("p k (o e) -> p k o e", e=2)
                                act.activation(v(swapped[n][i])[:, :, :, e], v(part[n][i])[:, :, :, 1 - e],
                                               ACT.Copy).then_inc(wswap, 1)
                    for half in range(2):
                        act.wait_ge(v_made, half + 1)
                        act.activation(v_all[:, half * 8:half * 8 + 8, :],
                                       c.psum[:, 6 + half, :].rearrange("p (t o) -> p t o", t=8), ACT.Copy,
                                       scale=1.0 / WSCALE).then_inc(v_done, 1)
                    act.wait_ge(v_done, 2)
                    with act.Fori(0, CH) as ch:
                        for m, (n, tile) in enumerate(jobs):
                            rows = 64 if n == "k" else P
                            tok = bass.ds(ch * BANK, BANK)
                            act.wait_ge(rope_done, ch * NJ + m + 1)
                            c.stand_alone(act)
                            dst = k_part[0][0:rows, tok] if n == "k" else q_part[0][:, tile, tok]
                            act.activation(dst, rope[0:rows, m, :], ACT.Copy).then_inc(hi_done, 1)

                @block.tensor
                def _(pe):
                    pe.wait_ge(wlo, 3)
                    for t in range(NT):
                        terms = [(k, a, w) for k in range(KT) for a, w in ((0, 0), (0, 1), (1, 0))]
                        for n, (k, a, w) in enumerate(terms):
                            last = pe.matmul(c.psum[:, 6 + t // 8, (t % 8) * 64:(t % 8) * 64 + 64],
                                             (c.xT_hi, c.xT_lo)[a][:, k, t * P:(t + 1) * P], part["v"][w][:, k, :],
                                             start=(n == 0), stop=(n == len(terms) - 1))
                        if t % 8 == 7:
                            last.then_inc(v_made, 1)
                    pe.wait_ge(wswap, 8)

                    def chunk(ch):
                        tok = bass.ds(ch * BANK, BANK)
                        for m, (n, tile) in enumerate(jobs):
                            rows = 64 if n == "k" else P
                            wait(pe, sin_done, (ch - 1) * NJ + m + 1)
                            c.stand_alone(pe)
                            for s, ww in enumerate((part, swapped)):
                                terms = [(k, w, a) for k in range(KT) for w, a in ((0, 0), (0, 1), (1, 0))]
                                for i, (k, w, a) in enumerate(terms):
                                    last = pe.matmul(c.psum[0:rows, 2 * m + s, :],
                                                     ww[n][w][:, k, tile * P:tile * P + rows],
                                                     (c.xT_hi, c.xT_lo)[a][:, k, tok],
                                                     start=(i == 0), stop=(i == len(terms) - 1))
                            last.then_inc(made, 1)

                    chunk(0)
                    with pe.Fori(1, CH) as ch:
                        chunk(ch)

                @block.vector
                def _(dve):
                    dve.wait_ge(loaded, 64)
                    for i, n in enumerate("qkvo"):
                        dve.wait_ge(whi, i + 1)
                        dve.scalar_tensor_tensor(out=part[n][1][:, :, :], in0=raw[n][:, :, :], scalar=WSCALE,
                                                 in1=part[n][0][:, :, :], op0=ALU.mult, op1=ALU.subtract).then_inc(wlo, 1)
                    dve.wait_ge(consts, 112)

                    def turn_job(ch, cb, m):
                        rows, pos = 64 if jobs[m][0] == "k" else P, slice(cb * BANK, (cb + 1) * BANK)
                        done = ch * NJ + m
                        dve.wait_ge(made, done + 1)
                        dve.tensor_tensor(tcos[0:rows, m, :], c.psum[0:rows, 2 * m, :], cos[0:rows, pos], ALU.mult).then_inc(cos_done, 1)
                        dve.tensor_tensor(tsin[0:rows, m, :], c.psum[0:rows, 2 * m + 1, :], sin[0:rows, pos], ALU.mult).then_inc(sin_done, 1)

                    def low_part(ch, m):
                        n, tile = jobs[m]
                        rows, tok = 64 if n == "k" else P, bass.ds(ch * BANK, BANK)
                        dve.wait_ge(hi_done, ch * NJ + m + 1)
                        hi_ = k_part[0][0:rows, tok] if n == "k" else q_part[0][:, tile, tok]
                        lo_ = k_part[1][0:rows, tok] if n == "k" else q_part[1][:, tile, tok]
                        dve.tensor_tensor(lo_, rope[0:rows, m, :], hi_, ALU.subtract).then_inc(lo_done, 1)

                    def chunk(ch, cb):
                        for m in range(NJ):
                            turn_job(ch, cb, m)
                            if m == 2:
                                low_part(ch, 0)
                            elif not (isinstance(ch, int) and ch == 0):
                                low_part(ch - 1, m + 1)

                    chunk(0, 0)
                    chunk(1, 1)
                    with dve.Fori(1, B) as b:
                        for cb in range(CB):
                            chunk(b * CB + cb, cb)
                    for m in range(1, NJ):
                        low_part(CH - 1, m)
                    dve.wait_ge(lo_done, CH * NJ)

        NP = 2 * J
        STEPS = [(kt, [j]) if kt * P < BANK else (kt, [j, j + 1]) for kt in range(TB)
                 for j in range(0, J, 1 if kt * P < BANK else 2)]
        SUB = len(STEPS)
        step_of = lambda kt: STEPS.index(next(s for s in STEPS if s[0] == kt))
        KEYS = [("kx", 0), ("kx", 1)]
        QS = [("qx", 0), ("qx", 1)]
        SCAN = []
        for t in range(TB):
            for p0 in range((t * P) // BANK + 1):
                n = min(BANK, (t + 1) * P - p0 * BANK)
                per = BANK // n if n <= BANK // 2 else 1
                per = J if n == P else per
                SCAN += [("scan", t, p0, j, per) for j in range(0, J, per)]
        MTS = [("mt", 0), ("mt", 1)]
        TURNS = [("ot", 0), ("ot", 1)]
        PREP = KEYS + QS + SCAN + MTS
        ALL = KEYS + QS + TURNS[:1] + SCAN[:8] + TURNS[1:] + SCAN[8:] + MTS

        def spread(items):
            price = [(TB - kt + 1) * len(heads) for kt, heads in STEPS]
            out, at, total = [], 0, sum(price)
            for s in range(SUB):
                upto = -(-len(items) * sum(price[:s + 1]) // total)
                out.append(items[at:upto])
                at = upto
            return out

        FIRST_UNIT, ANY_UNIT, LAST_UNIT = spread(PREP), spread(ALL), spread(TURNS)
        N_FIRST, N_HEAD = 2 * len(PREP) + len(ALL), 2 * len(ALL)
        assert N_FIRST % 2 == 0 and len(ALL) % 2 == 0

        with ExitStack() as actx:
            asb = lambda n, shape, dt=F32: c.sb(f"a1_{n}", shape, dt, actx)
            prob = asb("prob", [P, NP, S])
            o_sb = asb("o_sb", [P, 2, S])
            rsum = asb("rsum", [P, TB // 2, J])
            work_ready, work_free = [sem(f"work_ready{i}") for i in range(2)], [sem(f"work_free{i}") for i in range(2)]
            kd_ready, qp_ready, vg_ready, mcol_ready, qf_ready = (
                sem(n) for n in ("kd_ready", "qp_ready", "vg_ready", "mcol_ready", "qf_ready"))
            scores_ready, prob_ready, context_done, o_ready = (
                sem(n) for n in ("scores_ready", "prob_ready", "context_done", "o_ready"))
            rsum_ready, att_ready, turned = sem("rsum_ready"), sem("att_ready"), sem("turned")

            def work(slot, a, b_):
                return c.psum[:, 6 + slot, a:b_]

            def turn(number):
                return number[1] % 2, number[0] + number[1] // 2

            def run(eng, do_item, step=lambda *a: None, unit_end=None, before_item=None):
                def unit(g, b, number, steps):
                    for s in range(SUB):
                        step(2 * g + b, b, s)
                        for n, item in enumerate(steps[s]):
                            if before_item:
                                before_item(2 * g + b, b, s, n, len(steps[s]))
                            do_item(item, number, g, b)
                            number = (number[0], number[1] + 1)
                        if before_item:
                            before_item(2 * g + b, b, s, len(steps[s]), len(steps[s]))
                    if unit_end:
                        unit_end(2 * g + b, b)
                    return number

                number = (0, 0)
                for item in PREP:
                    do_item(item, number, -1, 1)
                    number = (0, number[1] + 1)
                number = unit(0, 0, number, FIRST_UNIT)
                number = unit(0, 1, number, ANY_UNIT)
                assert number[1] == N_FIRST
                with eng.Fori(1, G1 - 1) as g:
                    base = ((g - 1) * (N_HEAD // 2) + N_FIRST // 2, 0)
                    unit(g, 1, unit(g, 0, base, ANY_UNIT), ANY_UNIT)
                number = ((G1 - 2) * (N_HEAD // 2) + N_FIRST // 2, 0)
                number = unit(G1 - 1, 1, unit(G1 - 1, 0, number, ANY_UNIT), LAST_UNIT)
                for item in TURNS:
                    do_item(item, number, G1, 0)
                    number = (number[0], number[1] + 1)

            def at(index, n=1):
                return slice(index * n, index * n + n) if isinstance(index, int) else bass.ds(index * n, n)

            def n_mx(t):
                return sum(1 for i in SCAN if i[1] < t)

            with nc.Block() as block:
                @block.tensor
                def _(pe):
                    def do_item(item, number, g, b):
                        slot, before = turn(number)
                        wait(pe, work_free[slot], before)
                        wb, kind = 1 - b, item[0]
                        wg = g + 1 if b else g
                        w = 2 * g + b + 1
                        if kind == "kx":
                            tok = slice(wb * S + item[1] * BANK, wb * S + (item[1] + 1) * BANK)
                            for i in range(2):
                                last = pe.matmul(work(slot, 0, BANK), sel_k[i][:, at(wg), :], k_part[i][:, tok],
                                                 start=(i == 0), stop=(i == 1))
                        elif kind == "qx":
                            tok = slice(wb * S + item[1] * BANK, wb * S + (item[1] + 1) * BANK)
                            for n, (k, i) in enumerate([(k, i) for k in range(KT) for i in range(2)]):
                                last = pe.matmul(work(slot, 0, BANK), sel_q[i][:, k, at(wg), :], q_part[i][:, k, tok],
                                                 start=(n == 0), stop=(n == 2 * KT - 1))
                        elif kind == "scan":
                            _, t, p0, j0, per = item
                            pe.wait_ge(kd_ready, w * 2 * J + 2 * J)
                            pe.wait_ge(qp_ready, w * 2 + 2)
                            a, e = p0 * BANK, min((p0 + 1) * BANK, (t + 1) * P)
                            edge, n = e == (t + 1) * P, e - a
                            for i in range(per):
                                last = pe.matmul(work(slot, i * n, i * n + n), qp[:, wb, t * P:(t + 1) * P],
                                                 kd[:, wb, j0 + i, a:e], start=True, stop=not edge)
                                if edge:
                                    last = pe.matmul(work(slot, (i + 1) * n - P, (i + 1) * n), c.ident_b[:, :],
                                                     c.mask_qk[:, :], start=False, stop=True)
                        elif kind == "mt":
                            pe.wait_ge(mcol_ready, w * TB + 4 * item[1] + 4)
                            for i in range(4):
                                last = pe.matmul(work(slot, i * P, (i + 1) * P), mcol[:, 4 * item[1] + i, :], ident_h[:, :],
                                                 start=True, stop=True)
                        elif kind == "ot":
                            pe.wait_ge(o_ready, 2 * g + b)
                            for i in range(4):
                                last = pe.transpose(work(slot, i * P, (i + 1) * P),
                                                    o_sb[:, 1 - b, (4 * item[1] + i) * P:(4 * item[1] + i + 1) * P], c.ident[:, :])
                        last.then_inc(work_ready[slot], 1)

                    def make_scores(u, b, s):
                        kt, heads = STEPS[s]
                        if s == 0:
                            pe.wait_ge(qf_ready, u * 2 + 2)
                        wait(pe, prob_ready, u * SUB + s - 1)
                        for i, j in enumerate(heads):
                            for n, (a, e) in enumerate(spans(kt * P, S)):
                                bank = 2 * (s % 2) + (a // BANK if len(heads) == 1 else i)
                                scores = c.psum[:, bank, a % BANK:a % BANK + e - a]
                                last = pe.matmul(scores, kd[:, b, j, kt * P:(kt + 1) * P], qf[:, b, a:e],
                                                 start=True, stop=(n > 0))
                                if n == 0:
                                    last = pe.matmul(scores[:, 0:P], c.ident_b[:, :], c.mask_kq[:, :], start=False, stop=True)
                        last.then_inc(scores_ready, 1)

                    def before_item(u, b, s, i, n):
                        if s == 0 and i == min(1, n):
                            make_scores(u, b, 0)
                        if s + 1 < SUB and i == (min(2, n) if s == 0 else min(1, n)):
                            make_scores(u, b, s + 1)
                        kt, later = STEPS[s][0], s - step_of(STEPS[s][0])
                        if i == n and kt >= 1:
                            for part in range(2):
                                if later == (1 + 2 * part if kt * P < BANK else 1):
                                    make_context(u, b, kt - 1, part)
                        if i == n and s == SUB - 1:
                            make_context(u, b, TB - 1, 1)

                    def make_context(u, b, kt, part):
                        pieces = [(a, e) for a, e in spans(kt * P, S) if (e == S) == part]
                        if not pieces:
                            return
                        if len(list(spans(kt * P, S))) == 1 or not part:
                            pe.wait_ge(prob_ready, u * SUB + (step_of(kt + 1) if kt + 1 < TB else SUB))
                            pe.wait_ge(vg_ready, u + 1)
                        if kt == 0 and not part:
                            wait(pe, o_ready, u)
                        for a, e in pieces:
                            for i in range(J):
                                out = c.psum[i * R:(i + 1) * R, 4 + a // BANK, a % BANK:a % BANK + e - a]
                                last = pe.matmul(out, vg[:, b, kt, :], prob[:, J * (kt % 2) + i, a:e],
                                                 start=(kt == 0), stop=(kt == (e - 1) // P))
                        if part:
                            last.then_inc(context_done, 1)

                    run(pe, do_item, before_item=before_item)

                @block.scalar
                def _(act):
                    def do_item(item, number, g, b):
                        slot, before = turn(number)
                        wb, w = 1 - b, 2 * g + b + 1
                        if item[0] == "qx":
                            act.wait_ge(work_ready[slot], before + 1)
                            act.activation(qp[:, wb, item[1] * BANK:(item[1] + 1) * BANK], work(slot, 0, BANK),
                                           ACT.Copy).then_inc(qp_ready, 1)
                            act.wait_ge(qp_ready, w * 2 + item[1] + 1)
                            act.sem_inc(work_free[slot], 1)
                            if item[1] == 1:
                                wait(act, context_done, (w - 1) * TB)
                                wg = g + 1 if b else g
                                c.stand_alone(act)
                                act.activation(vg[:, wb, :, 0:HD1], v_all[:, wb * TB:(wb + 1) * TB, at(wg, HD1)],
                                               ACT.Copy).then_inc(vg_ready, 1)

                    def step(u, b, s):
                        kt, heads = STEPS[s]
                        act.wait_ge(scores_ready, u * SUB + s + 1)
                        wait(act, context_done, u * TB + kt - 1)
                        pair, at_ = c.psum[:, 2 * (s % 2):2 * (s % 2) + 2, :], J * (kt % 2) + heads[0]
                        if len(heads) == 1:
                            src, dst = pair.rearrange("p b n -> p (b n)")[:, kt * P:S], prob[:, at_, kt * P:S]
                        else:
                            src, dst = pair[:, :, kt * P - BANK:S - BANK], prob[:, at_:at_ + 2, kt * P:S]
                        act.activation(dst, src, ACT.Exp, scale=SCALE).then_inc(prob_ready, 1)

                    def unit_end(u, b):
                        act.wait_ge(context_done, u * TB + TB)
                        wait(act, turned, (u - 1) * 2)
                        act.activation(o_sb[:, b, :], c.psum[:, 4:6, :].rearrange("p b n -> p (b n)"),
                                       ACT.Copy).then_inc(o_ready, 1)

                    run(act, do_item, step, unit_end)

                @block.vector
                def _(dve):
                    def do_item(item, number, g, b):
                        slot, before = turn(number)
                        wb, w, kind = 1 - b, 2 * g + b + 1, item[0]
                        if kind == "qx":
                            return
                        dve.wait_ge(work_ready[slot], before + 1)
                        if kind == "kx":
                            i = item[1]
                            cols = slice(i * BANK, (i + 1) * BANK)
                            dve.tensor_copy(kp[:, i, :], work(slot, 0, BANK)).then_inc(work_free[slot], 1)
                            dve.wait_ge(work_free[slot], before + 1)
                            if i == 0:
                                wait(dve, scores_ready, (w - 1) * SUB)
                            for j in range(J):
                                rows = slice(j * R, (j + 1) * R)
                                dve.tensor_scalar(kd[rows, wb, j, cols], kp[rows, i, :], minus_row[rows, 0:1], None,
                                                  ALU.add).then_inc(kd_ready, 1)
                        elif kind == "scan":
                            _, t, p0, j0, per = item
                            a, e = p0 * BANK, min((p0 + 1) * BANK, (t + 1) * P)
                            n = e - a
                            index = SCAN.index(item)
                            if index == 0:
                                wait(dve, mcol_ready, w * TB)
                            dve.tensor_reduce(mx[:, t, j0:j0 + per, p0], work(slot, 0, per * n).rearrange("p (j n) -> p j n", j=per),
                                              AX.X, ALU.max).then_inc(work_free[slot], 1)
                            if index + 1 == n_mx(t + 1):
                                dve.wait_ge(work_free[slot], before + 1)
                                other, earlier = turn((number[0], number[1] - 1))
                                dve.wait_ge(work_free[other], earlier + 1)
                                dst = mcol[:, t, :].rearrange("p (j r) -> p j r", j=J)[:, :, 3 * HD1]
                                if t == 0:
                                    wait(dve, qf_ready, w * 2)
                                if t * P < BANK:
                                    dve.tensor_copy(dst, mx[:, t, :, 0]).then_inc(mcol_ready, 1)
                                else:
                                    dve.tensor_tensor(dst, mx[:, t, :, 0], mx[:, t, :, 1], ALU.max).then_inc(mcol_ready, 1)
                        elif kind == "mt":
                            i = item[1]
                            cols = slice(i * BANK, (i + 1) * BANK)
                            dve.tensor_tensor(qf[:, wb, cols], work(slot, 0, BANK), qp[:, wb, cols], ALU.add).then_inc(qf_ready, 1)
                            dve.wait_ge(qf_ready, w * 2 + i + 1)
                            dve.sem_inc(work_free[slot], 1)
                        elif kind == "ot":
                            i = item[1]
                            pu, pb = 2 * g + b - 1, 1 - b
                            v = work(slot, 0, BANK).rearrange("p (t j r) -> p t j r", t=4, j=J)
                            wait(dve, att_ready, pu * 2 + i)
                            dve.reciprocal(rsum[:, :, :], v[:, :, :, ONE]).then_inc(rsum_ready, 1)
                            dve.wait_ge(rsum_ready, pu * 2 + i + 1)
                            pg = g - 1 if b == 0 else g
                            dst = att[:, pb * TB + 4 * i:pb * TB + 4 * i + 4, at(pg, J * HD1)].rearrange("p t (j d) -> p t j d", j=J)
                            dve.tensor_tensor(dst, v[:, :, :, 0:HD1], rsum[:, :, :].unsqueeze(3).broadcast_to([P, 4, J, HD1]),
                                              ALU.mult).then_inc(att_ready, 1)
                            dve.wait_ge(att_ready, pu * 2 + i + 1)
                            dve.sem_inc(work_free[slot], 1)
                            dve.sem_inc(turned, 1)

                    run(dve, do_item)

        at_turned, at_hi, at_lo, y_made, y_out = (sem(n) for n in ("at_turned", "at_hi", "at_lo", "y_made", "y_out"))
        GRP, PER = 2, 4
        with nc.Block() as block:
            @block.tensor
            def _(pe):
                for m in range(NT // GRP):
                    wait(pe, at_lo, m - 1)
                    for j in range(GRP):
                        for k in range(KT):
                            last = pe.transpose(c.psum[:, m % 2, k * GRP * P + j * P:k * GRP * P + (j + 1) * P],
                                                att[:, m * GRP + j, k * P:(k + 1) * P], c.ident[:, :])
                    last.then_inc(at_turned, 1)
                pe.wait_ge(at_lo, NT // GRP)
                with pe.Fori(0, NT // PER) as i:
                    for j in range(PER):
                        for n, (k, w, a) in enumerate([(k, w, a) for k in range(KT) for w, a in ((0, 0), (0, 1), (1, 0))]):
                            last = pe.matmul(c.psum[:, 4 + j, 0:D], (c.xT_hi, c.xT_lo)[a][:, k, bass.ds((i * PER + j) * P, P)],
                                             wo_part[w][:, k, :], start=(n == 0), stop=(n == 3 * KT - 1))
                        last.then_inc(y_made, 1)
                    pe.wait_ge(y_out, i * PER + PER)

            @block.scalar
            def _(act):
                with act.Fori(0, NT // PER) as i:
                    for g in range(PER // GRP):
                        m = i * 2 + g
                        act.wait_ge(at_turned, m + 1)
                        c.stand_alone(act)
                        act.activation(c.xT_hi[:, :, bass.ds(m * GRP * P, GRP * P)],
                                       c.psum[:, g, :].rearrange("p (k n) -> p k n", k=KT), ACT.Copy).then_inc(at_hi, 1)
                with act.Fori(0, NT // PER) as i:
                    for j in range(PER):
                        t = i * PER + j
                        act.wait_ge(y_made, t + 1)
                        c.stand_alone(act)
                        act.activation(c.y[:, bass.ds(t, 1), :], c.psum[:, 4 + j:5 + j, 0:D], ACT.Copy, scale=1.0 / WSCALE).then_inc(y_out, 1)

            @block.vector
            def _(dve):
                with dve.Fori(0, NT // PER) as i:
                    for g in range(PER // GRP):
                        m = i * 2 + g
                        span = bass.ds(m * GRP * P, GRP * P)
                        dve.wait_ge(at_hi, m + 1)
                        dve.tensor_tensor(c.xT_lo[:, :, span], c.psum[:, g, :].rearrange("p (k n) -> p k n", k=KT),
                                          c.xT_hi[:, :, span], ALU.subtract).then_inc(at_lo, 1)


_INS = ["L0_attn_hidden_states", "L0_attn_Wq", "L0_attn_bq", "L0_attn_Wk", "L0_attn_bk", "L0_attn_Wv", "L0_attn_bv",
        "L0_attn_Wo", "L0_attn_bo", "L0_ffn_w1", "L0_ffn_w2", "L0_ffn_w3", "L1_attn_wq", "L1_attn_wk", "L1_attn_wv",
        "L1_attn_wo", "L1_ffn_w_gate", "L1_ffn_w_up", "L1_ffn_w_down"]


def shape_constants():
    import numpy as np

    def angles(width):
        exponent = np.arange(0, width, 2, dtype=np.float32) / np.float32(width)
        inv_freq = (np.float32(1.0) / np.power(np.float32(10000.0), exponent)).astype(np.float32)
        return np.arange(S, dtype=np.float32)[:, None] * inv_freq[None, :]

    a0 = angles(HD0).T
    tables = {
        "rope0_cos": np.concatenate([np.cos(a0)] * 2, 0),
        "rope0_sin": np.concatenate([np.sin(a0), -np.sin(a0)], 0),
    }
    a1 = np.repeat(angles(HD1).T, 2, 0)
    sign = np.where(np.arange(HD1) % 2 == 0, -1.0, 1.0).astype(np.float32)[:, None]
    tables["rope1_cos"] = np.tile(np.cos(a1), (P // HD1, 1)) / np.float32(WSCALE)
    tables["rope1_sin"] = np.tile(np.sin(a1) * sign, (P // HD1, 1)) / np.float32(WSCALE)
    tables = {k: np.ascontiguousarray(v, dtype=np.float32) for k, v in tables.items()}
    rep, rows = H1 // G1, P // (H1 // G1)
    sel_q = np.zeros((2, P, KT, G1, P), np.float16)
    sel_k = np.zeros((2, P, G1, P), np.float16)
    for g in range(G1):
        for j in range(rep):
            for d in range(HD1):
                q_row = (g * rep + j) * HD1 + d
                for copy, (q_part, k_part) in enumerate(((0, 0), (0, 1), (1, 0))):
                    sel_q[q_part, q_row % P, q_row // P, g, j * rows + copy * HD1 + d] = 1.0
                    sel_k[k_part, g * HD1 + d, g, j * rows + copy * HD1 + d] = 1.0
    tables["sel_q"], tables["sel_k"] = sel_q, sel_k
    minus = np.zeros((P, 1), np.float32)
    minus[3 * HD1::rows] = -1.0
    tables["minus_row"] = minus
    return tables


def kernel(**inputs):
    import numpy as _np
    import concourse.bacc as _bacc
    from concourse import mybir as _mybir
    from concourse.bass_utils import run_bass_kernel_spmd as _run

    nc = _bacc.Bacc("TRN2", target_bir_lowering=False, num_devices=1)
    arrays, args = {}, {}
    inputs = dict(inputs)
    for n in ("L0_attn_bq", "L0_attn_bk"):
        inputs[n] = _np.asarray(inputs[n]).reshape(H0, HD0).T
    for n in ("L0_attn_Wq", "L0_attn_Wk", "L0_attn_Wv", "L0_attn_Wo", "L0_ffn_w1", "L0_ffn_w2", "L0_ffn_w3",
              "L1_ffn_w_gate", "L1_ffn_w_up", "L1_ffn_w_down"):
        inputs[n] = _np.asarray(inputs[n]).T
    for name, a in list(inputs.items()) + list(shape_constants().items()):
        a = _np.ascontiguousarray(a)
        arrays[f"in_{name}_dram"] = a
        args[name] = nc.dram_tensor(f"in_{name}_dram", a.shape, _mybir.dt.from_np(a.dtype), kind="ExternalInput").ap()
    out = nc.dram_tensor("out_0_dram", (B, S, D), F32, kind="ExternalOutput").ap()
    program(nc, args, out)
    r = _run(nc, [arrays], core_ids=[0])
    return r.results[0]["out_0_dram"]
```
